# Optimizing a Trainium2 kernel written in Bass

```python
import numpy as np
import jax
import jax.numpy as jnp

def _softmax(x, axis=-1):
    return jax.nn.softmax(x, axis=axis)

def _gelu(x):
    return jax.nn.gelu(x, approximate=True)

def _silu(x):
    return jax.nn.silu(x)

def _sigmoid(x):
    return jax.nn.sigmoid(x)

def _layernorm(x, axis=-1, eps=1e-05):
    m = jnp.mean(x, axis=axis, keepdims=True)
    v = jnp.var(x, axis=axis, keepdims=True)
    return (x - m) / jnp.sqrt(v + eps)

def _scatter_add(tgt, idx, src, axis=0):
    return tgt.at[idx].add(src)

def _segment_sum(src, seg, n):
    return jax.ops.segment_sum(src, seg, n)
kernel_name = 'mk_xattn_ffn_d1_seqx_r4_c2f571'

def setup_inputs(seed: int=0):
    np.random.seed(seed)
    _w = jnp.asarray

    def _rec_inputs():
        import jax
        import jax.numpy as jnp
        _rk = jax.random.key(seed)
        x = -0.000125 + 0.9999 * jax.random.normal(jax.random.fold_in(_rk, 1), (8, 512, 512), jnp.float32)
        _lenS = 512 - jax.random.randint(jax.random.fold_in(_rk, 7), (8,), 0, max(1, 512 // 4) + 1, jnp.int32)
        _lenS2 = 64 - jax.random.randint(jax.random.fold_in(_rk, 8), (8,), 0, max(1, 64 // 4) + 1, jnp.int32)
        _ctx_2048P = jax.random.normal(jax.random.fold_in(_rk, 11), (8, 16, 512), jnp.float32)
        _ctx_2048c = jax.random.dirichlet(jax.random.fold_in(_rk, 511), 0.3 * jnp.ones((16,), jnp.float32), (8, 64))
        _ctx_2048t = jnp.einsum('bsk,bkd->bsd', _ctx_2048c, _ctx_2048P)
        _ctx_2048t = _ctx_2048t * jax.lax.rsqrt(jnp.mean(jnp.square(_ctx_2048t)) + 1e-12) * 0.953939
        ctx_2048 = 0.00222621 + 0.99962 * (_ctx_2048t + 0.3 * jax.random.normal(jax.random.fold_in(_rk, 611), (8, 64, 512), jnp.float32))
        itok_Sx4_0_63 = jax.random.randint(jax.random.fold_in(_rk, 12), (512, 4), 0, 64, jnp.int32)
        return (x, ctx_2048, itok_Sx4_0_63)
    x, ctx_2048, itok_Sx4_0_63 = _rec_inputs()

    def _L0_xattn_setup():
        import math
        import jax, jax.numpy as jnp
        import numpy as np
        B, S, D, N, K, TOPK = (4, 1024, 512, 64, 4, 2)
        key = jax.random.key(seed)
        k0, k1, k2, k3, k4 = jax.random.split(key, 5)
        token_states = jax.random.normal(k0, (B, S, D), dtype=jnp.float32)
        set_states = jax.random.normal(k1, (B, N, D), dtype=jnp.float32)
        desc_router = jax.random.normal(k2, (N, D), dtype=jnp.float32)
        token_to_sets = jax.random.randint(k3, (S, K), 0, N)
        bound = 1.0 / math.sqrt(D)
        W_q = jax.random.uniform(k4, (D, D), jnp.float32, -bound, bound)
        b_q = jnp.zeros((D,), jnp.float32)
        return {'token_states': token_states, 'set_states': set_states, 'desc_router': desc_router, 'W_q': W_q, 'b_q': b_q, 'token_to_sets': token_to_sets}
    _L0_xattn_all = _L0_xattn_setup()
    _L0_xattn_in = {k: v for k, v in _L0_xattn_all.items() if k in ('desc_router', 'W_q', 'b_q')}
    del _L0_xattn_all

    def _L0_ffn_setup():
        import jax, jax.numpy as jnp
        import numpy as np
        B, S, H, F, E, R, K = (2, 256, 512, 1792, 8, 32, 2)

        def _gather_slot(a_all, e):
            return jnp.take_along_axis(a_all, e[:, None, None], axis=1)[:, 0]
        key = jax.random.key(seed)
        ks = jax.random.split(key, 12)
        sc = 0.02
        n = lambda k, shape, s: jax.random.normal(k, shape, dtype=jnp.float32) * s
        return {'hidden_states': n(ks[0], (B, S, H), 1.0), 'Wg': n(ks[1], (E, H), sc), 'W1': n(ks[2], (F, H), sc), 'W2': n(ks[3], (H, F), sc), 'W3': n(ks[4], (F, H), sc), 'A1': n(ks[5], (E, R, H), sc), 'B1': n(ks[6], (E, F, R), sc), 'A2': n(ks[7], (E, R, F), sc), 'B2': n(ks[8], (E, H, R), sc), 'A3': n(ks[9], (E, R, H), sc), 'B3': n(ks[10], (E, F, R), sc)}
    _L0_ffn_all = _L0_ffn_setup()
    _L0_ffn_in = {k: v for k, v in _L0_ffn_all.items() if k in ('Wg', 'W1', 'W2', 'W3', 'A1', 'B1', 'A2', 'B2', 'A3', 'B3')}
    del _L0_ffn_all
    return {'x': x, 'ctx_2048': ctx_2048, 'itok_Sx4_0_63': itok_Sx4_0_63, 'L0_xattn_desc_router': _L0_xattn_in['desc_router'], 'L0_xattn_W_q': _L0_xattn_in['W_q'], 'L0_xattn_b_q': _L0_xattn_in['b_q'], 'L0_ffn_Wg': _L0_ffn_in['Wg'], 'L0_ffn_W1': _L0_ffn_in['W1'], 'L0_ffn_W2': _L0_ffn_in['W2'], 'L0_ffn_W3': _L0_ffn_in['W3'], 'L0_ffn_A1': _L0_ffn_in['A1'], 'L0_ffn_B1': _L0_ffn_in['B1'], 'L0_ffn_A2': _L0_ffn_in['A2'], 'L0_ffn_B2': _L0_ffn_in['B2'], 'L0_ffn_A3': _L0_ffn_in['A3'], 'L0_ffn_B3': _L0_ffn_in['B3']}

def reference(x, ctx_2048, itok_Sx4_0_63, L0_xattn_desc_router, L0_xattn_W_q, L0_xattn_b_q, L0_ffn_Wg, L0_ffn_W1, L0_ffn_W2, L0_ffn_W3, L0_ffn_A1, L0_ffn_B1, L0_ffn_A2, L0_ffn_B2, L0_ffn_A3, L0_ffn_B3):
    import jax
    import jax.numpy as jnp

    def _L0_xattn_ref(token_states, set_states, desc_router, W_q, b_q, token_to_sets):
        import math
        import jax, jax.numpy as jnp
        import numpy as np
        B, S, D, N, K, TOPK = (4, 1024, 512, 64, 4, 2)
        batch, seq_len, d = token_states.shape
        num_sets = set_states.shape[1]
        scale = 1.0 / math.sqrt(d)
        q = jnp.einsum('bsd,ed->bse', token_states, W_q) + b_q
        scores = jnp.einsum('bse,ne->bsn', q, desc_router) * scale
        valid = token_to_sets >= 0
        mask = ((token_to_sets[:, :, None] == jnp.arange(num_sets)[None, None, :]) & valid[:, :, None]).any(axis=1)
        neg_inf = jnp.array(-jnp.inf, scores.dtype)
        scores = jnp.where(mask[None, :, :], scores, neg_inf)
        topk_vals, topk_idx = jax.lax.top_k(scores, TOPK)
        b_i = jnp.arange(batch)[:, None, None]
        s_i = jnp.arange(seq_len)[None, :, None]
        scores = jnp.full_like(scores, neg_inf).at[b_i, s_i, topk_idx].set(topk_vals)
        weights = jax.nn.softmax(scores, axis=-1)
        return jnp.einsum('bsn,bnd->bsd', weights, set_states)

    def _L0_ffn_ref(hidden_states, Wg, W1, W2, W3, A1, B1, A2, B2, A3, B3):
        import jax, jax.numpy as jnp
        import numpy as np
        B, S, H, F, E, R, K = (2, 256, 512, 1792, 8, 32, 2)

        def _gather_slot(a_all, e):
            return jnp.take_along_axis(a_all, e[:, None, None], axis=1)[:, 0]
        b, s, h = hidden_states.shape
        x = hidden_states.reshape(-1, h)
        nE = Wg.shape[0]
        logits = x @ Wg.T
        probs = jax.nn.softmax(logits.astype(jnp.float32), axis=-1)
        rw, sel = jax.lax.top_k(probs, K)
        rw = (rw / rw.sum(axis=-1, keepdims=True)).astype(x.dtype)
        base1 = x @ W1.T
        base3 = x @ W3.T
        a1_all = jnp.einsum('th,erh->ter', x, A1)
        a3_all = jnp.einsum('th,erh->ter', x, A3)
        out = jnp.zeros_like(x)
        for k in range(K):
            e = sel[:, k]
            mask = jax.nn.one_hot(e, nE, dtype=x.dtype)
            a1 = _gather_slot(a1_all, e)
            a3 = _gather_slot(a3_all, e)
            lora1 = jnp.einsum('ter,efr->tf', mask[:, :, None] * a1[:, None, :], B1)
            lora3 = jnp.einsum('ter,efr->tf', mask[:, :, None] * a3[:, None, :], B3)
            x1 = base1 + lora1
            x3 = base3 + lora3
            x2 = jax.nn.silu(x1) * x3
            down = x2 @ W2.T
            a2_all = jnp.einsum('tf,erf->ter', x2, A2)
            a2 = _gather_slot(a2_all, e)
            lora2 = jnp.einsum('ter,ehr->th', mask[:, :, None] * a2[:, None, :], B2)
            out = out + (down + lora2) * rw[:, k:k + 1]
        return out.reshape(b, s, h)
    x = x + _L0_xattn_ref(_layernorm(x, axis=-1), ctx_2048, L0_xattn_desc_router, L0_xattn_W_q, L0_xattn_b_q, itok_Sx4_0_63)
    x = x + _L0_ffn_ref(_layernorm(x, axis=-1), L0_ffn_Wg, L0_ffn_W1, L0_ffn_W2, L0_ffn_W3, L0_ffn_A1, L0_ffn_B1, L0_ffn_A2, L0_ffn_B2, L0_ffn_A3, L0_ffn_B3)
    return x

_drawn_inputs = setup_inputs


def setup_inputs(seed=0):
    import zlib

    import numpy as np

    out = dict(_drawn_inputs(seed))
    spreads = {'L0_xattn_b_q': (0.0, 0.1)}
    factors = {'L0_ffn_Wg': 6.432,
     'L0_ffn_A1': 8.0,
     'L0_ffn_B1': 8.0,
     'L0_ffn_A2': 8.0,
     'L0_ffn_B2': 8.0,
     'L0_ffn_A3': 8.0,
     'L0_ffn_B3': 8.0}
    for name, (base, spread) in spreads.items():
        noise = np.random.default_rng([zlib.crc32(name.encode()), seed]).standard_normal(out[name].shape)
        drawn = base * np.exp(spread * noise) if base else spread * noise
        out[name] = jnp.asarray(drawn.astype(out[name].dtype))
    for name, factor in factors.items():
        out[name] = (out[name] * factor).astype(out[name].dtype)
    return out
```

```python
import concourse.bass as bass
from concourse import mybir
from contextlib import ExitStack

P = 128
B, S, H, F = 8, 512, 512, 1792
N, TOK = 64, 4
E, R = 8, 32
ER = E * R
KC = H // P
TT = S // P
FC = F // P
AC = ER // P
GROUPS = FC // 2
UPC = 2 * KC * P + 2 * AC * P
DNC = H + ER
WCOLS = UPC + DNC
LORA = 2 * KC * P
SELR = 32
EPS = 1e-5
FAR = 3.0e38
SCALE = float(H) ** -0.5

f32 = mybir.dt.float32
f32r = mybir.dt.float32r
i32 = mybir.dt.int32
u32 = mybir.dt.uint32
ALU = mybir.AluOpType
ACT = mybir.ActivationFunctionType


def build_front(nc, io, scratch, keep):
    w_scr, x1_scr, xt_scr, sel_scr = scratch
    A13h, A13l, B2h, B2l = keep
    with ExitStack() as ctx:
        def sb(name, shape, dt=f32):
            return ctx.enter_context(nc.sbuf_tensor(name, shape, dt))

        def sem(name):
            return ctx.enter_context(nc.semaphore(name))

        ident = sb("ident", [P, P])
        iota_set = sb("iota_set", [P, N])
        iota_exp = sb("iota_exp", [P, E])
        ones_row = sb("ones_row", [1, P])
        a_nat = sb("a_nat", [P, 2, AC, H])
        b2_nat = sb("b2_nat", [P, KC, E, R])
        wg_nat = sb("wg_nat", [E, H])
        desc_nat = sb("desc_nat", [N, H])
        wq_nat = sb("wq_nat", [P, KC, H])
        bq_nat = sb("bq_nat", [KC, P])
        bq_col = sb("bq_col", [P, KC])
        tok_i = sb("tok_i", [P, TT, TOK], i32)
        tok_f = sb("tok_f", [P, TT, TOK])
        member = sb("member", [P, TT, N])
        hit = sb("hit", [P, TT, N])
        penalty = sb("penalty", [P, TT, N])
        desc_t = sb("desc_t", [P, KC, N])
        wg_t = sb("wg_t", [P, KC, E])
        score_w = sb("score_w", [P, KC, N])
        score_b = sb("score_b", [1, N])

        w_nat = [sb(f"w_nat{j}", [P, WCOLS]) for j in range(2)]
        w_t = [sb(f"w_t{j}", [P, WCOLS]) for j in range(2)]

        x_in = sb("x_in", [P, TT, H])
        ctx_in = sb("ctx_in", [N, H])
        xn = sb("xn", [P, TT, H])
        xt = sb("xt", [P, KC, S])
        xt2 = sb("xt2", [P, KC, S])
        x1 = sb("x1", [P, TT, H])
        bn = sb("bn", [P, TT, 6])
        mv = sb("mv", [P, TT, 2])
        ve = sb("ve", [P, TT])
        sd = sb("sd", [P, TT])
        rs = sb("rs", [P, TT])
        nt = sb("nt", [P, TT])
        sc = sb("sc", [P, TT, N])
        best = sb("best", [P, TT, 8])
        bidx = sb("bidx", [P, TT, 8], u32)
        bidx_f = sb("bidx_f", [P, TT, 8])
        gap = sb("gap", [P, TT])
        eg = sb("eg", [P, TT])
        den = sb("den", [P, TT])
        w2v = sb("w2v", [P, 2, TT])
        oh = sb("oh", [P, 2, TT, N])
        wd = sb("wd", [P, TT, N])
        wd_t = sb("wd_t", [N, S])
        lg = sb("lg", [P, TT, E])
        sel = sb("sel", [P, TT, SELR])
        sel_t = sb("sel_t", [SELR, S])

        pt = [ctx.enter_context(nc.psum_tensor(f"pt{i}", [P, 512], f32)) for i in range(5)]
        pm = ctx.enter_context(nc.psum_tensor("pm", [P, 512], f32))
        pc = [ctx.enter_context(nc.psum_tensor(f"pc{i}", [P, 512], f32)) for i in range(2)]

        consts = sem("consts")
        small_in = sem("small_in")
        small_t = sem("small_t")
        small_hi = sem("small_hi")
        small_lo = sem("small_lo")
        sw_ready = sem("sw_ready")
        sw_done = sem("sw_done")
        nat_in = [sem(f"nat_in{j}") for j in range(2)]
        wt_ready = sem("wt_ready")
        wt_act = sem("wt_act")
        wt_dve = sem("wt_dve")
        ws_out = [sem(f"ws_out{j}") for j in range(2)]
        ws_wrap = sem("ws_wrap")
        dve = sem("dve")
        x_loaded = sem("x_loaded")
        ctx_loaded = sem("ctx_loaded")
        ve_done = sem("ve_done")
        sd_done = sem("sd_done")
        xn_done = sem("xn_done")
        xt_ready = sem("xt_ready")
        xt_done = sem("xt_done")
        sc_ready = sem("sc_ready")
        gap_done = sem("gap_done")
        eg_done = sem("eg_done")
        wd_done = sem("wd_done")
        wdt_ready = sem("wdt_ready")
        wdt_done = sem("wdt_done")
        mix_ready = sem("mix_ready")
        x1_done = sem("x1_done")
        x1_out = sem("x1_out")
        xt_out = sem("xt_out")
        sel_out = sem("sel_out")

        block = ctx.enter_context(nc.Block())

        NAT = [("W1", 0, H), ("W3", H, H), ("B1", 2 * H, ER), ("B3", 2 * H + ER, ER),
               ("W2", 2 * H + 2 * ER, H), ("A2", 3 * H + 2 * ER, ER)]

        def nat_loads(sp, j, c):
            w = w_nat[j]
            rows = bass.ds(c * P, P)
            for name, at, width in NAT:
                dst = w[:, at:at + width]
                if name in ("W1", "W3"):
                    src = io[name][rows, :]
                elif name in ("B1", "B3"):
                    src = io[name][:, rows, :].rearrange("e f r -> f e r")
                    dst = dst.rearrange("p (e r) -> p e r", e=E)
                elif name == "W2":
                    src = io[name][:, rows].rearrange("(k p) f -> p k f", p=P)
                    dst = dst.rearrange("p (k f) -> p k f", k=KC)
                else:
                    src = io[name].rearrange("e r f -> (e r) f")[:, rows].rearrange("(a p) f -> p a f", p=P)
                    dst = dst.rearrange("p (a f) -> p a f", a=AC)
                sp.dma_start(dst, src).then_inc(nat_in[j], 16)

        @block.sync
        def _(sp):
            for dst, src in (
                (a_nat[:, 0, :, :], io["A1"].rearrange("e r h -> (e r) h").rearrange("(a p) h -> p a h", p=P)),
                (a_nat[:, 1, :, :], io["A3"].rearrange("e r h -> (e r) h").rearrange("(a p) h -> p a h", p=P)),
                (b2_nat[:, 0, :, :], io["B2"][:, 0:P, :].rearrange("e p r -> p e r")),
                (b2_nat[:, 1, :, :], io["B2"][:, P:2 * P, :].rearrange("e p r -> p e r")),
                (b2_nat[:, 2, :, :], io["B2"][:, 2 * P:3 * P, :].rearrange("e p r -> p e r")),
                (b2_nat[:, 3, :, :], io["B2"][:, 3 * P:4 * P, :].rearrange("e p r -> p e r")),
                (wg_nat[:, :], io["Wg"]),
                (desc_nat[:, :], io["desc"]),
                (wq_nat[:, :, :], io["W_q"].rearrange("(k p) d -> p k d", p=P)),
                (bq_nat[:, :], io["b_q"].rearrange("(k p) -> k p", p=P)),
                (tok_i[:, :, :], io["tok"].rearrange("(i p) k -> p i k", p=P)),
            ):
                sp.dma_start(dst, src).then_inc(small_in, 16)
            for j in range(2):
                nat_loads(sp, j, j)

            def store_chunk(i, j):
                dst = w_scr[sp.snap(2 * i + j), :, :] if not isinstance(i, int) else w_scr[2 * i + j, :, :]
                na, nd = 6 * i + 3 * j + 3, 4 * i + 2 * j + 2
                if not isinstance(i, int):
                    na, nd = sp.snap(na), sp.snap(nd)
                sp.wait_ge(wt_act, na)
                sp.wait_ge(wt_dve, nd)
                sp.dma_start(dst, w_t[j][:, :]).then_inc(ws_out[j], 16)

            for i in range(GROUPS):
                for j in range(2):
                    store_chunk(i, j)
                    if i + 1 < GROUPS:
                        nat_loads(sp, j, 2 * (i + 1) + j)
            sp.wait_ge(ws_out[0], 16 * GROUPS)
            sp.dma_start(w_scr[FC, :, :], w_scr[0, :, :]).then_inc(ws_wrap, 16)

        @block.gpsimd
        def _(pool):
            pool.memset(ident[:, :], 0.0).then_inc(consts, 1)
            pool.wait_ge(consts, 1)
            pool.affine_select(out=ident[:, :], in_=ident[:, :], compare_op=ALU.not_equal, fill=1.0,
                               base=0, pattern=[[-1, P]], channel_multiplier=1).then_inc(consts, 1)
            pool.memset(ones_row[:, :], 1.0).then_inc(consts, 1)
            pool.memset(sel[:, :, :], 0.0).then_inc(consts, 1)
            pool.iota(iota_set[:, :], pattern=[[1, N]], base=0, channel_multiplier=0,
                      allow_small_or_imprecise_dtypes=True).then_inc(consts, 1)
            pool.iota(iota_exp[:, :], pattern=[[1, E]], base=0, channel_multiplier=0,
                      allow_small_or_imprecise_dtypes=True).then_inc(consts, 1)
            xr = io["x"].rearrange("b (i p) h -> b p i h", p=P)
            pool.dma_start(x_in[:, :, :], xr[0, :, :, :]).then_inc(x_loaded, 16)
            pool.dma_start(ctx_in[:, :], io["ctx"][0, :, :]).then_inc(ctx_loaded, 16)
            for b in range(B):
                pool.wait_ge(x1_done, TT * (b + 1))
                if b + 1 < B:
                    pool.dma_start(x_in[:, :, :], xr[b + 1, :, :, :]).then_inc(x_loaded, 16)
                    pool.dma_start(ctx_in[:, :], io["ctx"][b + 1, :, :]).then_inc(ctx_loaded, 16)
                pool.dma_start(x1_scr[b, :, :, :], x1[:, :, :]).then_inc(x1_out, 16)
                pool.wait_ge(xt_done, 2 * TT * (b + 1))
                pool.dma_start(xt_scr[b, :, :, :], xt2[:, :, :]).then_inc(xt_out, 16)
                pool.wait_ge(wdt_done, 2 * (b + 1))
                pool.dma_start(sel_scr[b, :, :], sel_t[:, :]).then_inc(sel_out, 16)
            for s, n in ((x1_out, B), (xt_out, B), (sel_out, B), (ws_wrap, 1), (ws_out[0], GROUPS),
                         (ws_out[1], GROUPS)):
                pool.wait_ge(s, 16 * n)

        @block.tensor
        def _(pe):
            pe.wait_ge(consts, 6)
            pe.wait_ge(small_in, 16 * 11)
            bank = 0
            for m in range(2):
                for half in range(2):
                    if bank >= 4:
                        pe.wait_ge(small_lo, bank - 3)
                    for kk in range(2):
                        for a in range(AC):
                            k = 2 * half + kk
                            mm = pe.transpose(pt[bank % 4][:, kk * ER + a * P:kk * ER + (a + 1) * P],
                                              a_nat[:, m, a, k * P:(k + 1) * P], ident[:, :])
                    mm.then_inc(small_t, 1)
                    bank += 1
            for a in range(AC):
                pe.wait_ge(small_lo, bank - 3)
                for k in range(KC):
                    mm = pe.transpose(pt[bank % 4][:, k * P:(k + 1) * P],
                                      b2_nat[:, k, 4 * a:4 * a + 4, :].rearrange("p e r -> p (e r)"), ident[:, :])
                mm.then_inc(small_t, 1)
                bank += 1
            pe.wait_ge(small_lo, bank - 3)
            for k in range(KC):
                pe.transpose(pt[bank % 4][:, k * N:(k + 1) * N], desc_nat[:, k * P:(k + 1) * P], ident[0:N, 0:N])
            for k in range(KC):
                pe.transpose(pt[bank % 4][:, KC * N + k * E:KC * N + (k + 1) * E],
                             wg_nat[:, k * P:(k + 1) * P], ident[0:E, 0:E])
            mm = pe.transpose(pt[bank % 4][:, KC * (N + E):KC * (N + E) + KC], bq_nat[:, :], ident[0:KC, 0:KC])
            mm.then_inc(small_t, 1)
            pe.wait_ge(small_lo, 7)
            for d in range(KC):
                for k in range(KC):
                    pe.matmul(pm[:, d * N:(d + 1) * N], wq_nat[:, k, d * P:(d + 1) * P], desc_t[:, k, :],
                              start=(k == 0), stop=(k == KC - 1))
            for k in range(KC):
                mm = pe.matmul(pm[0:1, KC * N:KC * N + N], bq_col[:, k:k + 1], desc_t[:, k, :],
                               start=(k == 0), stop=(k == KC - 1))
            mm.then_inc(sw_ready, 1)

            def chunk(i, j):
                pe.wait_ge(nat_in[j], 96 * (i + 1))
                c = 2 * i + j
                for t in range(5):
                    if c == 0:
                        if t == 0:
                            pe.wait_ge(sw_done, 1)
                    elif t % 2 == 0:
                        pe.wait_ge(wt_act, 3 * (c - 1) + t // 2 + 1)
                    else:
                        pe.wait_ge(wt_dve, 2 * (c - 1) + t // 2 + 1)
                    lo, hi = 512 * t, min(512 * (t + 1), WCOLS)
                    for q in range(lo, hi, P):
                        mm = pe.transpose(pt[t][:, q - lo:q - lo + P], w_nat[j][:, q:q + P], ident[:, :])
                    mm.then_inc(wt_ready, 1)

            def transposes(stage, b):
                for i in range(TT):
                    pe.wait_ge(xn_done, 2 * TT * b + stage * TT + i + 1)
                    if 2 * b + stage >= 1:
                        pe.wait_ge(xt_done, (2 * b + stage - 1) * TT + i + 1)
                    for k in range(KC):
                        mm = pe.transpose(pt[i][:, k * P:(k + 1) * P], xn[:, i, k * P:(k + 1) * P], ident[:, :])
                    mm.then_inc(xt_ready, 1)

            def front(b):
                transposes(0, b)
                for i in range(TT):
                    pe.wait_ge(xt_done, 2 * TT * b + i + 1)
                    for k in range(KC):
                        pe.matmul(pm[:, i * N:(i + 1) * N], xt[:, k, i * P:(i + 1) * P], score_w[:, k, :],
                                  start=(k == 0), stop=False)
                    mm = pe.matmul(pm[:, i * N:(i + 1) * N], ones_row[:, :], score_b[:, :], start=False, stop=True)
                mm.then_inc(sc_ready, 1)
                pe.wait_ge(wd_done, 2 * b + 1)
                if b >= 1:
                    pe.wait_ge(wdt_done, 2 * b)
                for i in range(TT):
                    mm = pe.transpose(pt[4][0:N, i * P:(i + 1) * P], wd[:, i, :], ident[:, :])
                mm.then_inc(wdt_ready, 1)
                pe.wait_ge(wdt_done, 2 * b + 1)
                pe.wait_ge(ctx_loaded, 16 * (b + 1))
                for i in range(TT):
                    if b * TT + i >= 2:
                        pe.wait_ge(x1_done, b * TT + i - 1)
                    pe.matmul(pc[i % 2][:, :], wd_t[:, i * P:(i + 1) * P], ctx_in[:, :], start=True, stop=True)\
                      .then_inc(mix_ready, 1)
                transposes(1, b)
                for i in range(TT):
                    pe.wait_ge(xt_done, 2 * TT * b + TT + i + 1)
                    for k in range(KC):
                        mm = pe.matmul(pm[:, i * E:(i + 1) * E], xt2[:, k, i * P:(i + 1) * P], wg_t[:, k, :],
                                       start=(k == 0), stop=(k == KC - 1))
                mm.then_inc(sc_ready, 1)
                pe.wait_ge(wd_done, 2 * b + 2)
                for i in range(TT):
                    mm = pe.transpose(pt[4][0:SELR, i * P:(i + 1) * P], sel[:, i, :], ident[:, :])
                mm.then_inc(wdt_ready, 1)

            for i in range(GROUPS):
                for j in range(2):
                    chunk(i, j)
            pe.wait_ge(wt_act, 3 * FC)
            pe.wait_ge(wt_dve, 2 * FC)
            for b in range(B):
                front(b)

        @block.scalar
        def _(act):
            for bank in range(6):
                act.wait_ge(small_t, bank + 1)
                if bank < 4:
                    dst = A13h[:, bank // 2, 2 * (bank % 2):2 * (bank % 2) + 2, :].rearrange("p k c -> p (k c)")
                else:
                    dst = B2h[:, bank - 4, :]
                act.activation(dst, pt[bank % 4][:, :], ACT.Copy).then_inc(small_hi, 1)
            for c in range(FC):
                i, j = c // 2, c % 2
                if i >= 1:
                    act.wait_ge(ws_out[j], 16 * i)
                for t in (0, 2, 4):
                    act.wait_ge(wt_ready, 5 * c + t + 1)
                    lo, hi = 512 * t, min(512 * (t + 1), WCOLS)
                    act.activation(w_t[j][:, lo:hi], pt[t][:, 0:hi - lo], ACT.Copy).then_inc(wt_act, 1)

            def root(n):
                act.wait_ge(ve_done, n)
                act.activation(sd[:, :], ve[:, :], ACT.Sqrt).then_inc(sd_done, 1)

            def take(stage, b):
                dst = xt2 if stage else xt
                if stage and b >= 1:
                    act.wait_ge(xt_out, 16 * b)
                for i in range(TT):
                    act.wait_ge(xt_ready, 2 * TT * b + stage * TT + i + 1)
                    act.activation(dst[:, :, i * P:(i + 1) * P], pt[i][:, :].rearrange("p (k t) -> p k t", k=KC),
                                   ACT.Copy).then_inc(xt_done, 1)

            def expo(n, scale):
                act.wait_ge(gap_done, n)
                act.activation(eg[:, :], gap[:, :], ACT.Exp, scale=scale).then_inc(eg_done, 1)

            for b in range(B):
                root(2 * b + 1)
                take(0, b)
                expo(2 * b + 1, SCALE)
                act.wait_ge(wdt_ready, 2 * b + 1)
                act.activation(wd_t[:, :], pt[4][0:N, :], ACT.Copy).then_inc(wdt_done, 1)
                root(2 * b + 2)
                take(1, b)
                expo(2 * b + 2, 1.0)
                act.wait_ge(wdt_ready, 2 * b + 2)
                if b >= 1:
                    act.wait_ge(sel_out, 16 * b)
                act.activation(sel_t[:, :], pt[4][0:SELR, :], ACT.Copy).then_inc(wdt_done, 1)

        @block.vector
        def _(v):
            steps = [0]

            def link(ins):
                steps[0] += 1
                ins.then_inc(dve, 1)
                v.wait_ge(dve, steps[0])

            for bank in range(6):
                v.wait_ge(small_hi, bank + 1)
                if bank < 4:
                    at = (slice(None), bank // 2, slice(2 * (bank % 2), 2 * (bank % 2) + 2), slice(None))
                    h, lo = A13h[at].rearrange("p k c -> p (k c)"), A13l[at].rearrange("p k c -> p (k c)")
                else:
                    h, lo = B2h[:, bank - 4, :], B2l[:, bank - 4, :]
                v.tensor_tensor(lo, pt[bank % 4][:, :], h.bitcast(f32), ALU.subtract).then_inc(small_lo, 1)
            v.wait_ge(small_t, 7)
            v.tensor_copy(desc_t[:, :, :], pt[2][:, 0:KC * N].rearrange("p (k n) -> p k n", k=KC))
            v.tensor_copy(bq_col[:, :], pt[2][:, KC * (N + E):KC * (N + E) + KC])
            v.tensor_copy(wg_t[:, :, :], pt[2][:, KC * N:KC * N + KC * E].rearrange("p (k n) -> p k n", k=KC))\
             .then_inc(small_lo, 1)
            v.wait_ge(sw_ready, 1)
            v.tensor_copy(score_w[:, :, :], pm[:, 0:KC * N].rearrange("p (k n) -> p k n", k=KC))
            v.tensor_copy(score_b[:, :], pm[0:1, KC * N:KC * N + N]).then_inc(sw_done, 1)
            v.wait_ge(consts, 6)
            v.wait_ge(small_in, 16 * 11)
            link(v.tensor_copy(tok_f[:, :, :], tok_i[:, :, :]))
            iota_b = iota_set[:, :].unsqueeze(1).to_broadcast([P, TT, N])
            for k in range(TOK):
                tok_b = tok_f[:, :, k:k + 1].to_broadcast([P, TT, N])
                link(v.tensor_tensor((hit if k else member)[:, :, :], iota_b, tok_b, ALU.is_equal))
                if k:
                    link(v.tensor_tensor(member[:, :, :], member[:, :, :], hit[:, :, :], ALU.max))
            link(v.tensor_scalar(penalty[:, :, :], member[:, :, :], 1.0, FAR, ALU.subtract, ALU.mult))

            for c in range(FC):
                i, j = c // 2, c % 2
                if i >= 1:
                    v.wait_ge(ws_out[j], 16 * i)
                for t in (1, 3):
                    v.wait_ge(wt_ready, 5 * c + t + 1)
                    v.tensor_copy(w_t[j][:, 512 * t:512 * (t + 1)], pt[t][:, :]).then_inc(wt_dve, 1)

            def norm(src, n):
                for i in range(TT):
                    ins = v.bn_stats(bn[:, i, :], src[:, i, :])
                link(ins)
                for i in range(TT):
                    ins = v.bn_aggr(mv[:, i, :], bn[:, i, :])
                link(ins)
                steps[0] += 1
                v.tensor_scalar(ve[:, :], mv[:, :, 1], EPS, None, ALU.add).then_inc(ve_done, 1)
                steps[0] -= 1
                v.wait_ge(sd_done, n)
                link(v.reciprocal(rs[:, :], sd[:, :]))
                link(v.tensor_tensor(nt[:, :], rs[:, :], rs[:, :], ALU.mult))
                link(v.tensor_tensor(nt[:, :], nt[:, :], ve[:, :], ALU.mult))
                link(v.tensor_scalar(nt[:, :], nt[:, :], -0.5, 1.5, ALU.mult, ALU.add))
                link(v.tensor_tensor(rs[:, :], rs[:, :], nt[:, :], ALU.mult))
                if n >= 2:
                    v.wait_ge(xt_ready, TT * (n - 1))
                for i in range(TT):
                    v.tensor_scalar(xn[:, i, :], src[:, i, :], mv[:, i, 0:1], rs[:, i:i + 1],
                                    ALU.subtract, ALU.mult).then_inc(xn_done, 1)

            def two_best(vals, iota, width, n, dst0, dst1):
                for i in range(TT):
                    ins = v.max(best[:, i, :], vals[:, i, :])
                link(ins)
                v.tensor_tensor(gap[:, :], best[:, :, 1], best[:, :, 0], ALU.subtract).then_inc(gap_done, 1)
                for i in range(TT):
                    ins = v.max_index(bidx[:, i, :], best[:, i, :], vals[:, i, :])
                link(ins)
                link(v.tensor_copy(bidx_f[:, :, :], bidx[:, :, :]))
                it = iota[:, :].unsqueeze(1).to_broadcast([P, TT, width])
                v.tensor_tensor(dst0, it, bidx_f[:, :, 0:1].to_broadcast([P, TT, width]), ALU.is_equal)
                link(v.tensor_tensor(dst1, it, bidx_f[:, :, 1:2].to_broadcast([P, TT, width]), ALU.is_equal))
                v.wait_ge(eg_done, n)
                link(v.tensor_scalar(den[:, :], eg[:, :], 1.0, None, ALU.add))
                link(v.reciprocal(w2v[:, 0, :], den[:, :]))
                link(v.tensor_tensor(w2v[:, 1, :], eg[:, :], w2v[:, 0, :], ALU.mult))

            for b in range(B):
                v.wait_ge(x_loaded, 16 * (b + 1))
                norm(x_in, 2 * b + 1)
                v.wait_ge(sc_ready, 2 * b + 1)
                link(v.tensor_tensor(sc[:, :, :], pm[:, 0:TT * N].rearrange("p (i n) -> p i n", i=TT),
                                     penalty[:, :, :], ALU.add))
                two_best(sc, iota_set, N, 2 * b + 1, oh[:, 0, :, :], oh[:, 1, :, :])
                for s in range(2):
                    ins = v.tensor_tensor(oh[:, s, :, :], oh[:, s, :, :],
                                          w2v[:, s, :].unsqueeze(2).to_broadcast([P, TT, N]), ALU.mult)
                link(ins)
                v.tensor_tensor(wd[:, :, :], oh[:, 0, :, :], oh[:, 1, :, :], ALU.add).then_inc(wd_done, 1)
                if b >= 1:
                    v.wait_ge(x1_out, 16 * b)
                for i in range(TT):
                    v.wait_ge(mix_ready, TT * b + i + 1)
                    v.tensor_tensor(x1[:, i, :], pc[i % 2][:, :], x_in[:, i, :], ALU.add).then_inc(x1_done, 1)
                v.wait_ge(x1_done, TT * (b + 1))
                norm(x1, 2 * b + 2)
                v.wait_ge(sc_ready, 2 * b + 2)
                link(v.tensor_copy(lg[:, :, :], pm[:, 0:TT * E].rearrange("p (i n) -> p i n", i=TT)))
                if b >= 1:
                    v.wait_ge(wdt_ready, 2 * b)
                two_best(lg, iota_exp, E, 2 * b + 2, sel[:, :, 0:E], sel[:, :, E:2 * E])
                v.tensor_tensor(sel[:, :, 2 * E:3 * E], sel[:, :, E:2 * E], sel[:, :, 0:E], ALU.subtract)
                v.tensor_copy(sel[:, :, 3 * E:3 * E + 2], w2v[:, :, :].rearrange("p s i -> p i s")).then_inc(wd_done, 1)


def build_ffn(nc, out, scratch, keep):
    w_scr, x1_scr, xt_scr, sel_scr = scratch
    A13h, A13l, B2h, B2l = keep
    with ExitStack() as ctx:
        def sb(name, shape, dt=f32):
            return ctx.enter_context(nc.sbuf_tensor(name, shape, dt))

        def sem(name):
            return ctx.enter_context(nc.semaphore(name))

        def pair(name, shape, dt=f32):
            return [sb(f"{name}{j}", shape, dt) for j in range(2)]

        up_raw, dn_raw = pair("up_raw", [P, UPC]), pair("dn_raw", [P, DNC])
        up_hi, up_lo = pair("up_hi", [P, UPC], f32r), pair("up_lo", [P, UPC], f32r)
        dn_hi, dn_lo = pair("dn_hi", [P, DNC], f32r), pair("dn_lo", [P, DNC], f32r)
        xt_raw = sb("xt_raw", [P, KC, S])
        xt_hi = sb("xt_hi", [P, KC, S], f32r)
        xt_lo = sb("xt_lo", [P, KC, S], f32r)
        am_hi = sb("am_hi", [P, 2, 2, AC, S], f32r)
        am_lo = sb("am_lo", [P, 2, 2, AC, S], f32r)
        mask = sb("mask", [P, 3, AC, S])
        rw = sb("rw", [P, 2, S])
        gate0, gate1 = pair("gate0_", [P, S]), pair("gate1_", [P, S])
        pq, sq = pair("pq", [P, S]), pair("sq", [P, S])
        p_hi, p_lo = pair("p_hi", [P, S], f32r), pair("p_lo", [P, S], f32r)
        s_hi, s_lo = pair("s_hi", [P, S], f32r), pair("s_lo", [P, S], f32r)
        credit = sb("credit", [P, 16])
        acc = sb("acc", [P, TT, H])
        g_acc = sb("g_acc", [P, 2, AC, S])

        x1p = [ctx.enter_context(nc.psum_tensor(f"x1p{j}", [P, S], f32)) for j in range(2)]
        x3p = [ctx.enter_context(nc.psum_tensor(f"x3p{j}", [P, S], f32)) for j in range(2)]
        dp = [ctx.enter_context(nc.psum_tensor(f"dp{i}", [P, 512], f32)) for i in range(4)]

        up_in = [sem(f"up_in{j}") for j in range(2)]
        dn_in = [sem(f"dn_in{j}") for j in range(2)]
        up_hi_done = [sem(f"up_hi_done{j}") for j in range(2)]
        dn_hi_done = [sem(f"dn_hi_done{j}") for j in range(2)]
        up_ready = [sem(f"up_ready{j}") for j in range(2)]
        dn_ready = [sem(f"dn_ready{j}") for j in range(2)]
        xt_in, xt_hi_done, xt_ready = sem("xt_in"), sem("xt_hi_done"), sem("xt_split")
        mask_in, acc_in = sem("mask_in"), sem("acc_in")
        dp_ready, dp_free = sem("dp_ready"), sem("dp_free")
        ah_done, al_done = sem("ah_done"), sem("al_done")
        am0, am1 = sem("am0"), sem("am1")
        x1a, x3a, x1b, x3b = sem("x1a"), sem("x3a"), sem("x1b"), sem("x3b")
        silu0, silu1 = sem("silu0"), sem("silu1")
        p_done, q_done, s_done = sem("p_done"), sem("q_done"), sem("s_done")
        ph, sh, pl, sl = sem("ph"), sem("sh"), sem("pl"), sem("sl")
        g_done, gh, gl = sem("g_done"), sem("gh"), sem("gl")
        g_zero, y_out = sem("g_zero"), sem("y_out")
        dve, dve_g = sem("dve2"), sem("dve_g")

        block = ctx.enter_context(nc.Block())

        DPB = 4 + 8 * GROUPS + 4
        MASK_DMAS = 3 * E + 2

        @block.sync
        def _(sp):
            def load(sem_free, need, dst, src, sem_in):
                need = sp.snap(need)
                sp.wait_ge(sem_free, need)
                sp.dma_start(dst, src).then_inc(sem_in, 16)

            sp.dma_start(up_raw[0][:, :], w_scr[0, :, 0:UPC]).then_inc(up_in[0], 16)
            with sp.Fori(0, B) as b:
                load(xt_ready, KC * b + 1, xt_raw[:, :, :], xt_scr[b, :, :, :], xt_in)
                need = sp.snap(AC * b + 1)
                sp.wait_ge(gl, need)
                for m in range(3):
                    for e in range(E):
                        a, r0 = e // (P // R), (e % (P // R)) * R
                        sp.dma_start(mask[r0:r0 + R, m, a, :], sel_scr[b, m * E + e, :].partition_broadcast(R))\
                          .then_inc(mask_in, 16)
                for s in range(2):
                    sp.dma_start(rw[:, s, :], sel_scr[b, 3 * E + s, :].partition_broadcast(P)).then_inc(mask_in, 16)
                load(y_out, 16 * b + 16, acc[:, :, :], x1_scr[b, :, :, :], acc_in)
                with sp.Fori(0, GROUPS) as g:
                    q1 = sp.snap(b * GROUPS + g + 1)
                    load(up_ready[1], q1, up_raw[1][:, :], w_scr[sp.snap(2 * g + 1), :, 0:UPC], up_in[1])
                    for j in range(2):
                        load(dn_ready[j], q1, dn_raw[j][:, :], w_scr[sp.snap(2 * g + j), :, UPC:WCOLS], dn_in[j])
                    load(up_ready[0], q1, up_raw[0][:, :], w_scr[sp.snap(2 * g + 2), :, 0:UPC], up_in[0])

        @block.gpsimd
        def _(pool):
            def up_split(j, n):
                pool.wait_ge(up_hi_done[j], n)
                pool.tensor_tensor(up_lo[j][:, :], up_raw[j][:, :], up_hi[j][:, :].bitcast(f32), ALU.subtract)\
                    .then_inc(up_ready[j], 1)

            def dn_split(j, n):
                pool.wait_ge(dn_hi_done[j], n)
                pool.tensor_tensor(dn_lo[j][:, :], dn_raw[j][:, :], dn_hi[j][:, :].bitcast(f32), ALU.subtract)\
                    .then_inc(dn_ready[j], 1)

            up_split(0, 1)
            with pool.Fori(0, B) as b:
                pool.wait_ge(gl, AC * b + 1)
                pool.wait_ge(mask_in, 16 * MASK_DMAS * (b + 1))
                for t in range(2 * AC):
                    m, a = t // AC, t % AC
                    pool.wait_ge(al_done, b * 2 * AC + (t + 1))
                    for dst, src in ((am_hi, gate0), (am_lo, gate1)):
                        ins = pool.tensor_tensor(dst[:, m, 1, a, :], src[t % 2][:, :], mask[:, 2, a, :], ALU.mult)
                    ins.then_inc(am1, 1)
                pool.memset(g_acc[:, :, :, :], 0.0).then_inc(g_zero, 1)
                with pool.Fori(0, GROUPS) as g:
                    q = b * GROUPS + g
                    up_split(1, q + 1)
                    up_split(0, q + 2)
                    dn_split(0, q + 1)
                    dn_split(1, q + 1)

        @block.scalar
        def _(act):
            def up_split(j, n):
                act.wait_ge(up_in[j], 16 * n)
                act.activation(up_hi[j][:, :], up_raw[j][:, :], ACT.Copy).then_inc(up_hi_done[j], 1)

            def dn_split(j, n):
                act.wait_ge(dn_in[j], 16 * n)
                act.activation(dn_hi[j][:, :], dn_raw[j][:, :], ACT.Copy).then_inc(dn_hi_done[j], 1)

            def group(b, g):
                q = b * GROUPS + g
                n = q * 2
                for j in range(2):
                    act.wait_ge(x1a, n + (j + 1))
                    act.activation(gate0[j][:, :], x1p[j][:, :], ACT.Silu).then_inc(silu0, 1)
                    if j == 0:
                        up_split(1, q + 1)
                    act.wait_ge(x1b, n + (j + 1))
                    act.activation(gate1[j][:, :], x1p[j][:, :], ACT.Silu).then_inc(silu1, 1)
                    if j == 0:
                        act.wait_ge(dp_ready, b * DPB + g * 8 + 4)
                    act.wait_ge(p_done, n + (j + 1))
                    act.activation(p_hi[j][:, :], pq[j][:, :], ACT.Copy).then_inc(ph, 1)
                    act.wait_ge(s_done, n + (j + 1))
                    act.activation(s_hi[j][:, :], sq[j][:, :], ACT.Copy).then_inc(sh, 1)
                    if j == 0:
                        up_split(0, q + 2)
                        dn_split(0, q + 1)
                        dn_split(1, q + 1)

            up_split(0, 1)
            with act.Fori(0, B) as b:
                act.wait_ge(xt_in, 16 * (b + 1))
                for k in range(KC):
                    act.activation(xt_hi[:, k, :], xt_raw[:, k, :], ACT.Copy).then_inc(xt_hi_done, 1)
                for t in range(2 * AC):
                    act.wait_ge(dp_ready, b * DPB + (t + 1))
                    if t >= 2:
                        act.wait_ge(am0, b * 2 * AC + (t - 1))
                        act.wait_ge(am1, b * 2 * AC + (t - 1))
                    act.activation(gate0[t % 2][:, :].bitcast(f32r), dp[t][:, :], ACT.Copy).then_inc(ah_done, 1)
                act.wait_ge(am1, 2 * AC * (b + 1))
                with act.Fori(0, GROUPS) as g:
                    group(b, g)
                for a in range(AC):
                    act.wait_ge(g_done, b * AC + (a + 1))
                    act.activation((p_hi, s_hi)[a][0][:, :], g_acc[:, 0, a, :], ACT.Copy).then_inc(gh, 1)
                act.wait_ge(dp_free, b * DPB + (DPB + 4))
                act.dma_start(out[b, :, :].rearrange("(i p) h -> p i h", p=P), acc[:, :, :]).then_inc(y_out, 16)
            act.wait_ge(y_out, 16 * B + 16)

        @block.vector
        def _(v):
            v.memset(credit[:, 0:1], 0.0).then_inc(dp_free, 4)
            v.memset(credit[:, 1:2], 0.0).then_inc(silu1, 2)
            v.memset(credit[:, 2:3], 0.0).then_inc(q_done, 2)
            v.memset(credit[:, 3:4], 0.0).then_inc(up_ready[1], 1)
            v.memset(credit[:, 4:5], 0.0).then_inc(dn_ready[0], 1)
            v.memset(credit[:, 5:6], 0.0).then_inc(dn_ready[1], 1)
            v.memset(credit[:, 6:7], 0.0).then_inc(gl, 1)
            v.memset(credit[:, 7:8], 0.0).then_inc(xt_ready, 1)
            v.memset(credit[:, 8:9], 0.0).then_inc(y_out, 16)

            def down_adds(b, g):
                v.wait_ge(g_zero, b + 1)
                v.wait_ge(acc_in, 16 * (b + 1))
                for t in range(8):
                    v.wait_ge(dp_ready, b * DPB + g * 8 + (4 + t + 1))
                    to = acc[:, t, :] if t < TT else g_acc[:, (t - TT) // AC, (t - TT) % AC, :]
                    v.tensor_tensor(to, dp[t % 4][:, :], to, ALU.add).then_inc(dp_free, 1)

            def group(b, g, down):
                n = b * FC + g * 2
                for j in range(2):
                    v.wait_ge(silu0, n + (j + 1))
                    v.tensor_tensor(gate0[j][:, :], gate0[j][:, :], rw[:, 0, :], ALU.mult).then_inc(dve, 1)
                    v.wait_ge(dve, n * 2 + (2 * j + 1))
                    v.wait_ge(x3a, n + (j + 1))
                    v.tensor_tensor(pq[j][:, :], x3p[j][:, :], gate0[j][:, :], ALU.mult).then_inc(p_done, 1)
                    if down and j == 0:
                        down_adds(b, g - 1)
                    v.wait_ge(silu1, n + (j + 3))
                    v.tensor_tensor(gate1[j][:, :], gate1[j][:, :], rw[:, 1, :], ALU.mult).then_inc(dve, 1)
                    v.wait_ge(dve, n * 2 + (2 * j + 2))
                    v.wait_ge(x3b, n + (j + 1))
                    v.tensor_tensor(sq[j][:, :], x3p[j][:, :], gate1[j][:, :], ALU.mult).then_inc(q_done, 1)
                    v.wait_ge(q_done, n + (j + 3))
                    v.tensor_tensor(sq[j][:, :], sq[j][:, :], pq[j][:, :], ALU.add).then_inc(s_done, 1)
                    v.wait_ge(ph, n + (j + 1))
                    v.tensor_tensor(p_lo[j][:, :], pq[j][:, :], p_hi[j][:, :].bitcast(f32), ALU.subtract)\
                     .then_inc(pl, 1)
                    v.wait_ge(sh, n + (j + 1))
                    v.tensor_tensor(s_lo[j][:, :], sq[j][:, :], s_hi[j][:, :].bitcast(f32), ALU.subtract)\
                     .then_inc(sl, 1)

            with v.Fori(0, B) as b:
                for k in range(KC):
                    v.wait_ge(xt_hi_done, b * KC + (k + 1))
                    v.tensor_tensor(xt_lo[:, k, :], xt_raw[:, k, :], xt_hi[:, k, :].bitcast(f32), ALU.subtract)\
                     .then_inc(xt_ready, 1)
                v.wait_ge(mask_in, 16 * MASK_DMAS * (b + 1))
                for t in range(2 * AC):
                    m, a = t // AC, t % AC
                    v.wait_ge(ah_done, b * 2 * AC + (t + 1))
                    v.tensor_tensor(gate1[t % 2][:, :].bitcast(f32r), dp[t][:, :], gate0[t % 2][:, :], ALU.subtract)\
                     .then_inc(dp_free, 1)
                    v.tensor_tensor(am_hi[:, m, 0, a, :], gate0[t % 2][:, :], mask[:, 0, a, :], ALU.mult)\
                     .then_inc(al_done, 1)
                    v.wait_ge(al_done, b * 2 * AC + (t + 1))
                    v.tensor_tensor(am_lo[:, m, 0, a, :], gate1[t % 2][:, :], mask[:, 0, a, :], ALU.mult)\
                     .then_inc(am0, 1)
                group(b, 0, False)
                with v.Fori(1, GROUPS) as g:
                    group(b, g, True)
                down_adds(b, GROUPS - 1)
                v.wait_ge(dp_free, b * DPB + (4 + 4 + 8 * GROUPS))
                for a in range(AC):
                    v.tensor_tensor(g_acc[:, 0, a, :], g_acc[:, 0, a, :], mask[:, 1, a, :], ALU.mult)
                    ins = v.tensor_tensor(g_acc[:, 1, a, :], g_acc[:, 1, a, :], mask[:, 2, a, :], ALU.mult)
                ins.then_inc(dve_g, 1)
                v.wait_ge(dve_g, b + 1)
                for a in range(AC):
                    v.tensor_tensor(g_acc[:, 0, a, :], g_acc[:, 0, a, :], g_acc[:, 1, a, :], ALU.subtract)\
                     .then_inc(g_done, 1)
                for a in range(AC):
                    v.wait_ge(gh, b * AC + (a + 1))
                    ins = v.tensor_tensor((p_lo, s_lo)[a][0][:, :], g_acc[:, 0, a, :],
                                          (p_hi, s_hi)[a][0][:, :].bitcast(f32), ALU.subtract).then_inc(gl, 1)
                for i in range(TT):
                    v.wait_ge(dp_ready, b * DPB + (DPB - TT + i + 1))
                    v.tensor_tensor(acc[:, i, :], dp[i][:, :], acc[:, i, :], ALU.add).then_inc(dp_free, 1)

        @block.tensor
        def _(pe):
            def product(dst, pairs, start, stop, group_open=False):
                for x, (lh, ll, rh, rl) in enumerate(pairs):
                    for y, (lhs, rhs) in enumerate(((lh, rh), (lh, rl), (ll, rh))):
                        mm = pe.matmul(dst, lhs, rhs, start=start and x == 0 and y == 0,
                                       stop=stop and x == len(pairs) - 1 and y == 2, skip_group_check=True)
                return mm

            def base(j, m):
                at = m * KC * P
                return [(up_hi[j][:, at + k * P:at + (k + 1) * P], up_lo[j][:, at + k * P:at + (k + 1) * P],
                         xt_hi[:, k, :], xt_lo[:, k, :]) for k in range(KC)]

            def lora(j, m, s):
                at = LORA + m * AC * P
                return [(up_hi[j][:, at + a * P:at + (a + 1) * P], up_lo[j][:, at + a * P:at + (a + 1) * P],
                         am_hi[:, m, s, a, :], am_lo[:, m, s, a, :]) for a in range(AC)]

            def down(b, g):
                q = b * GROUPS + g
                pe.wait_ge(sl, q * 2 + 2)
                for j in range(2):
                    pe.wait_ge(dn_ready[j], q + 2)
                for t in range(8):
                    pe.wait_ge(dp_free, b * DPB + g * 8 + (4 + t + 1))
                    pairs = []
                    for j in range(2):
                        if t < TT:
                            c = slice(t * P, (t + 1) * P)
                            pairs.append((s_hi[j][:, c], s_lo[j][:, c], dn_hi[j][:, 0:H], dn_lo[j][:, 0:H]))
                        else:
                            a = (t - TT) % AC
                            c = slice(H + a * P, H + (a + 1) * P)
                            hi, lo = (s_hi, s_lo) if t < TT + AC else (p_hi, p_lo)
                            pairs.append((dn_hi[j][:, c], dn_lo[j][:, c], hi[j][:, :], lo[j][:, :]))
                    mm = product(dp[t % 4][:, :], pairs, True, True)
                    mm.then_inc(dp_ready, 1)

            def group(b, g, with_down):
                q = b * GROUPS + g
                n = q * 2
                for j in range(2):
                    first = isinstance(g, int) and j == 0
                    pe.wait_ge(up_ready[j], q + (1 + j))
                    pe.wait_ge(silu1, n + (j + 1))
                    product(x1p[j][:, :], base(j, 0), True, False)
                    if first:
                        pe.wait_ge(am0, b * 2 * AC + AC)
                    product(x1p[j][:, :], lora(j, 0, 0), False, True).then_inc(x1a, 1)
                    pe.wait_ge(q_done, n + (j + 1))
                    product(x3p[j][:, :], base(j, 1), True, False)
                    if first:
                        pe.wait_ge(am0, b * 2 * AC + 2 * AC)
                    product(x3p[j][:, :], lora(j, 1, 0), False, True).then_inc(x3a, 1)
                    if with_down and j == 0:
                        down(b, g - 1)
                    pe.wait_ge(silu0, n + (j + 1))
                    if first:
                        pe.wait_ge(am1, b * 2 * AC + 2 * AC)
                    product(x1p[j][:, :], lora(j, 0, 1), False, True).then_inc(x1b, 1)
                    pe.wait_ge(p_done, n + (j + 1))
                    product(x3p[j][:, :], lora(j, 1, 1), False, True).then_inc(x3b, 1)

            with pe.Fori(0, B) as b:
                for t in range(2 * AC):
                    m, a = t // AC, t % AC
                    if t == 0:
                        pe.wait_ge(xt_ready, b * KC + (KC + 1))
                    pe.wait_ge(dp_free, b * DPB + (t + 1))
                    c = slice(a * P, (a + 1) * P)
                    product(dp[t][:, :], [(A13h[:, m, k, c], A13l[:, m, k, c], xt_hi[:, k, :], xt_lo[:, k, :])
                                          for k in range(KC)], True, True).then_inc(dp_ready, 1)
                group(b, 0, False)
                with pe.Fori(1, GROUPS) as g:
                    group(b, g, True)
                down(b, GROUPS - 1)
                pe.wait_ge(gl, AC * b + (AC + 1))
                for i in range(TT):
                    pe.wait_ge(dp_free, b * DPB + (DPB - TT + i + 1))
                    c = slice(i * P, (i + 1) * P)
                    product(dp[i][:, :], [(hi[0][:, c], lo[0][:, c], B2h[:, a, :], B2l[:, a, :])
                                          for a, (hi, lo) in enumerate(((p_hi, p_lo), (s_hi, s_lo)))],
                            True, True).then_inc(dp_ready, 1)


def build(nc, io, out):
    def dram(name, shape):
        return nc.dram_tensor(name, shape, f32, kind="Internal").ap()

    scratch = (dram("w_scr", (FC + 1, P, WCOLS)), dram("x1_scr", (B, P, TT, H)),
               dram("xt_scr", (B, P, KC, S)), dram("sel_scr", (B, SELR, S)))
    with (nc.sbuf_tensor("A13h", [P, 2, KC, ER], f32r) as A13h, nc.sbuf_tensor("A13l", [P, 2, KC, ER], f32r) as A13l,
          nc.sbuf_tensor("B2h", [P, AC, H], f32r) as B2h, nc.sbuf_tensor("B2l", [P, AC, H], f32r) as B2l):
        keep = (A13h, A13l, B2h, B2l)
        build_front(nc, io, scratch, keep)
        build_ffn(nc, out, scratch, keep)


_INS = {"x": "x", "ctx_2048": "ctx", "itok_Sx4_0_63": "tok", "L0_xattn_desc_router": "desc", "L0_xattn_W_q": "W_q",
        "L0_xattn_b_q": "b_q", "L0_ffn_Wg": "Wg", "L0_ffn_W1": "W1", "L0_ffn_W2": "W2", "L0_ffn_W3": "W3",
        "L0_ffn_A1": "A1", "L0_ffn_B1": "B1", "L0_ffn_A2": "A2", "L0_ffn_B2": "B2", "L0_ffn_A3": "A3",
        "L0_ffn_B3": "B3"}


def kernel(**inputs):
    import numpy as _np
    import concourse.bacc as _bacc
    from concourse import mybir as _mybir
    from concourse.bass_utils import run_bass_kernel_spmd as _run

    nc = _bacc.Bacc("TRN2", target_bir_lowering=False, num_devices=1)
    arrays, io = {}, {}
    for name, short in _INS.items():
        a = _np.ascontiguousarray(inputs[name])
        arrays[f"in_{name}"] = a
        io[short] = nc.dram_tensor(f"in_{name}", a.shape, _mybir.dt.from_np(a.dtype), kind="ExternalInput").ap()
    out = nc.dram_tensor("out_0", (B, S, H), _mybir.dt.float32, kind="ExternalOutput").ap()
    build(nc, io, out)
    r = _run(nc, [arrays], core_ids=[0])
    return r.results[0]["out_0"]
```

```python
import concourse.bass as bass
from concourse import mybir
from contextlib import ExitStack

P = 128
B, S, H, F = 8, 512, 512, 1792
N, TOK = 64, 4
E, R = 8, 32
ER = E * R
KC = H // P
TT = S // P
FC = F // P
AC = ER // P
GROUPS = FC // 2
UPC = 2 * KC * P + 2 * AC * P
DNC = H + ER
WCOLS = UPC + DNC
LORA = 2 * KC * P
SELR = 32
EPS = 1e-5
FAR = 3.0e38
SCALE = float(H) ** -0.5

f32 = mybir.dt.float32
f32r = mybir.dt.float32r
i32 = mybir.dt.int32
u32 = mybir.dt.uint32
ALU = mybir.AluOpType
ACT = mybir.ActivationFunctionType


def build_front(nc, io, scratch, keep):
    w_scr, x1_scr, xt_scr, sel_scr = scratch
    A13h, A13l, B2h, B2l = keep
    with ExitStack() as ctx:
        def sb(name, shape, dt=f32):
            return ctx.enter_context(nc.sbuf_tensor(name, shape, dt))

        def sem(name):
            return ctx.enter_context(nc.semaphore(name))

        ident = sb("ident", [P, P])
        iota_set = sb("iota_set", [P, N])
        iota_exp = sb("iota_exp", [P, E])
        ones_row = sb("ones_row", [1, P])
        a_nat = sb("a_nat", [P, 2, AC, H])
        b2_nat = sb("b2_nat", [P, KC, E, R])
        wg_nat = sb("wg_nat", [E, H])
        desc_nat = sb("desc_nat", [N, H])
        wq_nat = sb("wq_nat", [P, KC, H])
        bq_nat = sb("bq_nat", [KC, P])
        bq_col = sb("bq_col", [P, KC])
        tok_i = sb("tok_i", [P, TT, TOK], i32)
        tok_f = sb("tok_f", [P, TT, TOK])
        member = sb("member", [P, TT, N])
        hit = sb("hit", [P, TT, N])
        penalty = sb("penalty", [P, TT, N])
        desc_t = sb("desc_t", [P, KC, N])
        wg_t = sb("wg_t", [P, KC, E])
        score_w = sb("score_w", [P, KC, N])
        score_b = sb("score_b", [1, N])

        w_nat = [sb(f"w_nat{j}", [P, WCOLS]) for j in range(2)]
        w_t = [sb(f"w_t{j}", [P, WCOLS]) for j in range(2)]

        x_in = sb("x_in", [P, TT, H])
        ctx_in = sb("ctx_in", [N, H])
        xn = sb("xn", [P, TT, H])
        xt = sb("xt", [P, KC, S])
        xt2 = sb("xt2", [P, KC, S])
        x1 = sb("x1", [P, TT, H])
        bn = sb("bn", [P, TT, 6])
        mv = sb("mv", [P, TT, 2])
        ve = sb("ve", [P, TT])
        sd = sb("sd", [P, TT])
        rs = sb("rs", [P, TT])
        nt = sb("nt", [P, TT])
        sc = sb("sc", [P, TT, N])
        best = sb("best", [P, TT, 8])
        bidx = sb("bidx", [P, TT, 8], u32)
        bidx_f = sb("bidx_f", [P, TT, 8])
        gap = sb("gap", [P, TT])
        eg = sb("eg", [P, TT])
        den = sb("den", [P, TT])
        w2v = sb("w2v", [P, 2, TT])
        oh = sb("oh", [P, 2, TT, N])
        wd = sb("wd", [P, TT, N])
        wd_t = sb("wd_t", [N, S])
        lg = sb("lg", [P, TT, E])
        sel = sb("sel", [P, TT, SELR])
        sel_t = sb("sel_t", [SELR, S])

        pt = [ctx.enter_context(nc.psum_tensor(f"pt{i}", [P, 512], f32)) for i in range(5)]
        pm = ctx.enter_context(nc.psum_tensor("pm", [P, 512], f32))
        pc = [ctx.enter_context(nc.psum_tensor(f"pc{i}", [P, 512], f32)) for i in range(2)]

        consts = sem("consts")
        small_in = sem("small_in")
        small_t = sem("small_t")
        small_hi = sem("small_hi")
        small_lo = sem("small_lo")
        sw_ready = sem("sw_ready")
        sw_done = sem("sw_done")
        nat_in = [sem(f"nat_in{j}") for j in range(2)]
        wt_ready = sem("wt_ready")
        wt_act = sem("wt_act")
        wt_dve = sem("wt_dve")
        ws_out = [sem(f"ws_out{j}") for j in range(2)]
        ws_wrap = sem("ws_wrap")
        dve = sem("dve")
        x_loaded = sem("x_loaded")
        ctx_loaded = sem("ctx_loaded")
        ve_done = sem("ve_done")
        sd_done = sem("sd_done")
        xn_done = sem("xn_done")
        xt_ready = sem("xt_ready")
        xt_done = sem("xt_done")
        sc_ready = sem("sc_ready")
        gap_done = sem("gap_done")
        eg_done = sem("eg_done")
        wd_done = sem("wd_done")
        wdt_ready = sem("wdt_ready")
        wdt_done = sem("wdt_done")
        mix_ready = sem("mix_ready")
        x1_done = sem("x1_done")
        x1_out = sem("x1_out")
        xt_out = sem("xt_out")
        sel_out = sem("sel_out")

        block = ctx.enter_context(nc.Block())

        NAT = [("W1", 0, H), ("W3", H, H), ("B1", 2 * H, ER), ("B3", 2 * H + ER, ER),
               ("W2", 2 * H + 2 * ER, H), ("A2", 3 * H + 2 * ER, ER)]

        def nat_loads(sp, j, c):
            w = w_nat[j]
            rows = bass.ds(c * P, P)
            for name, at, width in NAT:
                dst = w[:, at:at + width]
                if name in ("W1", "W3"):
                    src = io[name][rows, :]
                elif name in ("B1", "B3"):
                    src = io[name][:, rows, :].rearrange("e f r -> f e r")
                    dst = dst.rearrange("p (e r) -> p e r", e=E)
                elif name == "W2":
                    src = io[name][:, rows].rearrange("(k p) f -> p k f", p=P)
                    dst = dst.rearrange("p (k f) -> p k f", k=KC)
                else:
                    src = io[name].rearrange("e r f -> (e r) f")[:, rows].rearrange("(a p) f -> p a f", p=P)
                    dst = dst.rearrange("p (a f) -> p a f", a=AC)
                sp.dma_start(dst, src).then_inc(nat_in[j], 16)

        @block.sync
        def _(sp):
            for dst, src in (
                (a_nat[:, 0, :, :], io["A1"].rearrange("e r h -> (e r) h").rearrange("(a p) h -> p a h", p=P)),
                (a_nat[:, 1, :, :], io["A3"].rearrange("e r h -> (e r) h").rearrange("(a p) h -> p a h", p=P)),
                (b2_nat[:, 0, :, :], io["B2"][:, 0:P, :].rearrange("e p r -> p e r")),
                (b2_nat[:, 1, :, :], io["B2"][:, P:2 * P, :].rearrange("e p r -> p e r")),
                (b2_nat[:, 2, :, :], io["B2"][:, 2 * P:3 * P, :].rearrange("e p r -> p e r")),
                (b2_nat[:, 3, :, :], io["B2"][:, 3 * P:4 * P, :].rearrange("e p r -> p e r")),
                (wg_nat[:, :], io["Wg"]),
                (desc_nat[:, :], io["desc"]),
                (wq_nat[:, :, :], io["W_q"].rearrange("(k p) d -> p k d", p=P)),
                (bq_nat[:, :], io["b_q"].rearrange("(k p) -> k p", p=P)),
                (tok_i[:, :, :], io["tok"].rearrange("(i p) k -> p i k", p=P)),
            ):
                sp.dma_start(dst, src).then_inc(small_in, 16)
            for j in range(2):
                nat_loads(sp, j, j)

            def store_chunk(i, j):
                dst = w_scr[sp.snap(2 * i + j), :, :] if not isinstance(i, int) else w_scr[2 * i + j, :, :]
                na, nd = 6 * i + 3 * j + 3, 4 * i + 2 * j + 2
                if not isinstance(i, int):
                    na, nd = sp.snap(na), sp.snap(nd)
                sp.wait_ge(wt_act, na)
                sp.wait_ge(wt_dve, nd)
                sp.dma_start(dst, w_t[j][:, :]).then_inc(ws_out[j], 16)

            for i in range(GROUPS):
                for j in range(2):
                    store_chunk(i, j)
                    if i + 1 < GROUPS:
                        nat_loads(sp, j, 2 * (i + 1) + j)
            sp.wait_ge(ws_out[0], 16 * GROUPS)
            sp.dma_start(w_scr[FC, :, :], w_scr[0, :, :]).then_inc(ws_wrap, 16)

        @block.gpsimd
        def _(pool):
            pool.memset(ident[:, :], 0.0).then_inc(consts, 1)
            pool.wait_ge(consts, 1)
            pool.affine_select(out=ident[:, :], in_=ident[:, :], compare_op=ALU.not_equal, fill=1.0,
                               base=0, pattern=[[-1, P]], channel_multiplier=1).then_inc(consts, 1)
            pool.memset(ones_row[:, :], 1.0).then_inc(consts, 1)
            pool.memset(sel[:, :, :], 0.0).then_inc(consts, 1)
            pool.iota(iota_set[:, :], pattern=[[1, N]], base=0, channel_multiplier=0,
                      allow_small_or_imprecise_dtypes=True).then_inc(consts, 1)
            pool.iota(iota_exp[:, :], pattern=[[1, E]], base=0, channel_multiplier=0,
                      allow_small_or_imprecise_dtypes=True).then_inc(consts, 1)
            xr = io["x"].rearrange("b (i p) h -> b p i h", p=P)
            pool.dma_start(x_in[:, :, :], xr[0, :, :, :]).then_inc(x_loaded, 16)
            pool.dma_start(ctx_in[:, :], io["ctx"][0, :, :]).then_inc(ctx_loaded, 16)
            for b in range(B):
                pool.wait_ge(x1_done, TT * (b + 1))
                if b + 1 < B:
                    pool.dma_start(x_in[:, :, :], xr[b + 1, :, :, :]).then_inc(x_loaded, 16)
                    pool.dma_start(ctx_in[:, :], io["ctx"][b + 1, :, :]).then_inc(ctx_loaded, 16)
                pool.dma_start(x1_scr[b, :, :, :], x1[:, :, :]).then_inc(x1_out, 16)
                pool.wait_ge(xt_done, 2 * TT * (b + 1))
                pool.dma_start(xt_scr[b, :, :, :], xt2[:, :, :]).then_inc(xt_out, 16)
                pool.wait_ge(wdt_done, 2 * (b + 1))
                pool.dma_start(sel_scr[b, :, :], sel_t[:, :]).then_inc(sel_out, 16)
            for s, n in ((x1_out, B), (xt_out, B), (sel_out, B), (ws_wrap, 1), (ws_out[0], GROUPS),
                         (ws_out[1], GROUPS)):
                pool.wait_ge(s, 16 * n)

        @block.tensor
        def _(pe):
            pe.wait_ge(consts, 6)
            pe.wait_ge(small_in, 16 * 11)
            bank = 0
            for m in range(2):
                for half in range(2):
                    if bank >= 4:
                        pe.wait_ge(small_lo, bank - 3)
                    for kk in range(2):
                        for a in range(AC):
                            k = 2 * half + kk
                            mm = pe.transpose(pt[bank % 4][:, kk * ER + a * P:kk * ER + (a + 1) * P],
                                              a_nat[:, m, a, k * P:(k + 1) * P], ident[:, :])
                    mm.then_inc(small_t, 1)
                    bank += 1
            for a in range(AC):
                pe.wait_ge(small_lo, bank - 3)
                for k in range(KC):
                    mm = pe.transpose(pt[bank % 4][:, k * P:(k + 1) * P],
                                      b2_nat[:, k, 4 * a:4 * a + 4, :].rearrange("p e r -> p (e r)"), ident[:, :])
                mm.then_inc(small_t, 1)
                bank += 1
            pe.wait_ge(small_lo, bank - 3)
            for k in range(KC):
                pe.transpose(pt[bank % 4][:, k * N:(k + 1) * N], desc_nat[:, k * P:(k + 1) * P], ident[0:N, 0:N])
            for k in range(KC):
                pe.transpose(pt[bank % 4][:, KC * N + k * E:KC * N + (k + 1) * E],
                             wg_nat[:, k * P:(k + 1) * P], ident[0:E, 0:E])
            mm = pe.transpose(pt[bank % 4][:, KC * (N + E):KC * (N + E) + KC], bq_nat[:, :], ident[0:KC, 0:KC])
            mm.then_inc(small_t, 1)
            pe.wait_ge(small_lo, 7)
            for d in range(KC):
                for k in range(KC):
                    pe.matmul(pm[:, d * N:(d + 1) * N], wq_nat[:, k, d * P:(d + 1) * P], desc_t[:, k, :],
                              start=(k == 0), stop=(k == KC - 1))
            for k in range(KC):
                mm = pe.matmul(pm[0:1, KC * N:KC * N + N], bq_col[:, k:k + 1], desc_t[:, k, :],
                               start=(k == 0), stop=(k == KC - 1))
            mm.then_inc(sw_ready, 1)

            def chunk(i, j):
                pe.wait_ge(nat_in[j], 96 * (i + 1))
                c = 2 * i + j
                for t in range(5):
                    if c == 0:
                        if t == 0:
                            pe.wait_ge(sw_done, 1)
                    elif t % 2 == 0:
                        pe.wait_ge(wt_act, 3 * (c - 1) + t // 2 + 1)
                    else:
                        pe.wait_ge(wt_dve, 2 * (c - 1) + t // 2 + 1)
                    lo, hi = 512 * t, min(512 * (t + 1), WCOLS)
                    for q in range(lo, hi, P):
                        mm = pe.transpose(pt[t][:, q - lo:q - lo + P], w_nat[j][:, q:q + P], ident[:, :])
                    mm.then_inc(wt_ready, 1)

            def transposes(stage, b):
                for i in range(TT):
                    pe.wait_ge(xn_done, 2 * TT * b + stage * TT + i + 1)
                    if 2 * b + stage >= 1:
                        pe.wait_ge(xt_done, (2 * b + stage - 1) * TT + i + 1)
                    for k in range(KC):
                        mm = pe.transpose(pt[i][:, k * P:(k + 1) * P], xn[:, i, k * P:(k + 1) * P], ident[:, :])
                    mm.then_inc(xt_ready, 1)

            def front(b):
                transposes(0, b)
                for i in range(TT):
                    pe.wait_ge(xt_done, 2 * TT * b + i + 1)
                    for k in range(KC):
                        pe.matmul(pm[:, i * N:(i + 1) * N], xt[:, k, i * P:(i + 1) * P], score_w[:, k, :],
                                  start=(k == 0), stop=False)
                    mm = pe.matmul(pm[:, i * N:(i + 1) * N], ones_row[:, :], score_b[:, :], start=False, stop=True)
                mm.then_inc(sc_ready, 1)
                pe.wait_ge(wd_done, 2 * b + 1)
                if b >= 1:
                    pe.wait_ge(wdt_done, 2 * b)
                for i in range(TT):
                    mm = pe.transpose(pt[4][0:N, i * P:(i + 1) * P], wd[:, i, :], ident[:, :])
                mm.then_inc(wdt_ready, 1)
                pe.wait_ge(wdt_done, 2 * b + 1)
                pe.wait_ge(ctx_loaded, 16 * (b + 1))
                for i in range(TT):
                    if b * TT + i >= 2:
                        pe.wait_ge(x1_done, b * TT + i - 1)
                    pe.matmul(pc[i % 2][:, :], wd_t[:, i * P:(i + 1) * P], ctx_in[:, :], start=True, stop=True)\
                      .then_inc(mix_ready, 1)
                transposes(1, b)
                for i in range(TT):
                    pe.wait_ge(xt_done, 2 * TT * b + TT + i + 1)
                    for k in range(KC):
                        mm = pe.matmul(pm[:, i * E:(i + 1) * E], xt2[:, k, i * P:(i + 1) * P], wg_t[:, k, :],
                                       start=(k == 0), stop=(k == KC - 1))
                mm.then_inc(sc_ready, 1)
                pe.wait_ge(wd_done, 2 * b + 2)
                for i in range(TT):
                    mm = pe.transpose(pt[4][0:SELR, i * P:(i + 1) * P], sel[:, i, :], ident[:, :])
                mm.then_inc(wdt_ready, 1)

            for i in range(GROUPS):
                for j in range(2):
                    chunk(i, j)
            pe.wait_ge(wt_act, 3 * FC)
            pe.wait_ge(wt_dve, 2 * FC)
            for b in range(B):
                front(b)

        @block.scalar
        def _(act):
            for bank in range(6):
                act.wait_ge(small_t, bank + 1)
                if bank < 4:
                    dst = A13h[:, bank // 2, 2 * (bank % 2):2 * (bank % 2) + 2, :].rearrange("p k c -> p (k c)")
                else:
                    dst = B2h[:, bank - 4, :]
                act.activation(dst, pt[bank % 4][:, :], ACT.Copy).then_inc(small_hi, 1)
            for c in range(FC):
                i, j = c // 2, c % 2
                if i >= 1:
                    act.wait_ge(ws_out[j], 16 * i)
                for t in (0, 2, 4):
                    act.wait_ge(wt_ready, 5 * c + t + 1)
                    lo, hi = 512 * t, min(512 * (t + 1), WCOLS)
                    act.activation(w_t[j][:, lo:hi], pt[t][:, 0:hi - lo], ACT.Copy).then_inc(wt_act, 1)

            def root(n):
                act.wait_ge(ve_done, n)
                act.activation(sd[:, :], ve[:, :], ACT.Sqrt).then_inc(sd_done, 1)

            def take(stage, b):
                dst = xt2 if stage else xt
                if stage and b >= 1:
                    act.wait_ge(xt_out, 16 * b)
                for i in range(TT):
                    act.wait_ge(xt_ready, 2 * TT * b + stage * TT + i + 1)
                    act.activation(dst[:, :, i * P:(i + 1) * P], pt[i][:, :].rearrange("p (k t) -> p k t", k=KC),
                                   ACT.Copy).then_inc(xt_done, 1)

            def expo(n, scale):
                act.wait_ge(gap_done, n)
                act.activation(eg[:, :], gap[:, :], ACT.Exp, scale=scale).then_inc(eg_done, 1)

            for b in range(B):
                root(2 * b + 1)
                take(0, b)
                expo(2 * b + 1, SCALE)
                act.wait_ge(wdt_ready, 2 * b + 1)
                act.activation(wd_t[:, :], pt[4][0:N, :], ACT.Copy).then_inc(wdt_done, 1)
                root(2 * b + 2)
                take(1, b)
                expo(2 * b + 2, 1.0)
                act.wait_ge(wdt_ready, 2 * b + 2)
                if b >= 1:
                    act.wait_ge(sel_out, 16 * b)
                act.activation(sel_t[:, :], pt[4][0:SELR, :], ACT.Copy).then_inc(wdt_done, 1)

        @block.vector
        def _(v):
            steps = [0]

            def link(ins):
                steps[0] += 1
                ins.then_inc(dve, 1)
                v.wait_ge(dve, steps[0])

            for bank in range(6):
                v.wait_ge(small_hi, bank + 1)
                if bank < 4:
                    at = (slice(None), bank // 2, slice(2 * (bank % 2), 2 * (bank % 2) + 2), slice(None))
                    h, lo = A13h[at].rearrange("p k c -> p (k c)"), A13l[at].rearrange("p k c -> p (k c)")
                else:
                    h, lo = B2h[:, bank - 4, :], B2l[:, bank - 4, :]
                v.tensor_tensor(lo, pt[bank % 4][:, :], h.bitcast(f32), ALU.subtract).then_inc(small_lo, 1)
            v.wait_ge(small_t, 7)
            v.tensor_copy(desc_t[:, :, :], pt[2][:, 0:KC * N].rearrange("p (k n) -> p k n", k=KC))
            v.tensor_copy(bq_col[:, :], pt[2][:, KC * (N + E):KC * (N + E) + KC])
            v.tensor_copy(wg_t[:, :, :], pt[2][:, KC * N:KC * N + KC * E].rearrange("p (k n) -> p k n", k=KC))\
             .then_inc(small_lo, 1)
            v.wait_ge(sw_ready, 1)
            v.tensor_copy(score_w[:, :, :], pm[:, 0:KC * N].rearrange("p (k n) -> p k n", k=KC))
            v.tensor_copy(score_b[:, :], pm[0:1, KC * N:KC * N + N]).then_inc(sw_done, 1)
            v.wait_ge(consts, 6)
            v.wait_ge(small_in, 16 * 11)
            link(v.tensor_copy(tok_f[:, :, :], tok_i[:, :, :]))
            iota_b = iota_set[:, :].unsqueeze(1).to_broadcast([P, TT, N])
            for k in range(TOK):
                tok_b = tok_f[:, :, k:k + 1].to_broadcast([P, TT, N])
                link(v.tensor_tensor((hit if k else member)[:, :, :], iota_b, tok_b, ALU.is_equal))
                if k:
                    link(v.tensor_tensor(member[:, :, :], member[:, :, :], hit[:, :, :], ALU.max))
            link(v.tensor_scalar(penalty[:, :, :], member[:, :, :], 1.0, FAR, ALU.subtract, ALU.mult))

            for c in range(FC):
                i, j = c // 2, c % 2
                if i >= 1:
                    v.wait_ge(ws_out[j], 16 * i)
                for t in (1, 3):
                    v.wait_ge(wt_ready, 5 * c + t + 1)
                    v.tensor_copy(w_t[j][:, 512 * t:512 * (t + 1)], pt[t][:, :]).then_inc(wt_dve, 1)

            def norm(src, n):
                for i in range(TT):
                    ins = v.bn_stats(bn[:, i, :], src[:, i, :])
                link(ins)
                for i in range(TT):
                    ins = v.bn_aggr(mv[:, i, :], bn[:, i, :])
                link(ins)
                steps[0] += 1
                v.tensor_scalar(ve[:, :], mv[:, :, 1], EPS, None, ALU.add).then_inc(ve_done, 1)
                steps[0] -= 1
                v.wait_ge(sd_done, n)
                link(v.reciprocal(rs[:, :], sd[:, :]))
                link(v.tensor_tensor(nt[:, :], rs[:, :], rs[:, :], ALU.mult))
                link(v.tensor_tensor(nt[:, :], nt[:, :], ve[:, :], ALU.mult))
                link(v.tensor_scalar(nt[:, :], nt[:, :], -0.5, 1.5, ALU.mult, ALU.add))
                link(v.tensor_tensor(rs[:, :], rs[:, :], nt[:, :], ALU.mult))
                if n >= 2:
                    v.wait_ge(xt_ready, TT * (n - 1))
                for i in range(TT):
                    v.tensor_scalar(xn[:, i, :], src[:, i, :], mv[:, i, 0:1], rs[:, i:i + 1],
                                    ALU.subtract, ALU.mult).then_inc(xn_done, 1)

            def two_best(vals, iota, width, n, dst0, dst1):
                for i in range(TT):
                    ins = v.max(best[:, i, :], vals[:, i, :])
                link(ins)
                v.tensor_tensor(gap[:, :], best[:, :, 1], best[:, :, 0], ALU.subtract).then_inc(gap_done, 1)
                for i in range(TT):
                    ins = v.max_index(bidx[:, i, :], best[:, i, :], vals[:, i, :])
                link(ins)
                link(v.tensor_copy(bidx_f[:, :, :], bidx[:, :, :]))
                it = iota[:, :].unsqueeze(1).to_broadcast([P, TT, width])
                v.tensor_tensor(dst0, it, bidx_f[:, :, 0:1].to_broadcast([P, TT, width]), ALU.is_equal)
                link(v.tensor_tensor(dst1, it, bidx_f[:, :, 1:2].to_broadcast([P, TT, width]), ALU.is_equal))
                v.wait_ge(eg_done, n)
                link(v.tensor_scalar(den[:, :], eg[:, :], 1.0, None, ALU.add))
                link(v.reciprocal(w2v[:, 0, :], den[:, :]))
                link(v.tensor_tensor(w2v[:, 1, :], eg[:, :], w2v[:, 0, :], ALU.mult))

            for b in range(B):
                v.wait_ge(x_loaded, 16 * (b + 1))
                norm(x_in, 2 * b + 1)
                v.wait_ge(sc_ready, 2 * b + 1)
                link(v.tensor_tensor(sc[:, :, :], pm[:, 0:TT * N].rearrange("p (i n) -> p i n", i=TT),
                                     penalty[:, :, :], ALU.add))
                two_best(sc, iota_set, N, 2 * b + 1, oh[:, 0, :, :], oh[:, 1, :, :])
                for s in range(2):
                    ins = v.tensor_tensor(oh[:, s, :, :], oh[:, s, :, :],
                                          w2v[:, s, :].unsqueeze(2).to_broadcast([P, TT, N]), ALU.mult)
                link(ins)
                v.tensor_tensor(wd[:, :, :], oh[:, 0, :, :], oh[:, 1, :, :], ALU.add).then_inc(wd_done, 1)
                if b >= 1:
                    v.wait_ge(x1_out, 16 * b)
                for i in range(TT):
                    v.wait_ge(mix_ready, TT * b + i + 1)
                    v.tensor_tensor(x1[:, i, :], pc[i % 2][:, :], x_in[:, i, :], ALU.add).then_inc(x1_done, 1)
                v.wait_ge(x1_done, TT * (b + 1))
                norm(x1, 2 * b + 2)
                v.wait_ge(sc_ready, 2 * b + 2)
                link(v.tensor_copy(lg[:, :, :], pm[:, 0:TT * E].rearrange("p (i n) -> p i n", i=TT)))
                if b >= 1:
                    v.wait_ge(wdt_ready, 2 * b)
                two_best(lg, iota_exp, E, 2 * b + 2, sel[:, :, 0:E], sel[:, :, E:2 * E])
                v.tensor_tensor(sel[:, :, 2 * E:3 * E], sel[:, :, E:2 * E], sel[:, :, 0:E], ALU.subtract)
                v.tensor_copy(sel[:, :, 3 * E:3 * E + 2], w2v[:, :, :].rearrange("p s i -> p i s")).then_inc(wd_done, 1)


def build_ffn(nc, out, scratch, keep):
    w_scr, x1_scr, xt_scr, sel_scr = scratch
    A13h, A13l, B2h, B2l = keep
    with ExitStack() as ctx:
        def sb(name, shape, dt=f32):
            return ctx.enter_context(nc.sbuf_tensor(name, shape, dt))

        def sem(name):
            return ctx.enter_context(nc.semaphore(name))

        def pair(name, shape, dt=f32):
            return [sb(f"{name}{j}", shape, dt) for j in range(2)]

        up_raw, dn_raw = pair("up_raw", [P, UPC]), pair("dn_raw", [P, DNC])
        up_hi, up_lo = pair("up_hi", [P, UPC], f32r), pair("up_lo", [P, UPC], f32r)
        dn_hi, dn_lo = pair("dn_hi", [P, DNC], f32r), pair("dn_lo", [P, DNC], f32r)
        xt_raw = sb("xt_raw", [P, KC, S])
        xt_hi = sb("xt_hi", [P, KC, S], f32r)
        xt_lo = sb("xt_lo", [P, KC, S], f32r)
        am_hi = sb("am_hi", [P, 2, 2, AC, S], f32r)
        am_lo = sb("am_lo", [P, 2, 2, AC, S], f32r)
        mask_a = sb("mask_a", [P, 2, AC, S])
        mask_g = sb("mask_g", [P, 2, AC, S])
        rw = sb("rw", [P, 2, S])
        gate0, gate1 = pair("gate0_", [P, S]), pair("gate1_", [P, S])
        pq, sq = pair("pq", [P, S]), pair("sq", [P, S])
        p_hi, p_lo = pair("p_hi", [P, S], f32r), pair("p_lo", [P, S], f32r)
        s_hi, s_lo = pair("s_hi", [P, S], f32r), pair("s_lo", [P, S], f32r)
        g_hi, g_lo = p_hi, p_lo
        credit = sb("credit", [P, 16])
        acc = sb("acc", [P, TT, H])
        g_acc = sb("g_acc", [P, 2, AC, S])

        x1p = [ctx.enter_context(nc.psum_tensor(f"x1p{j}", [P, S], f32)) for j in range(2)]
        x3p = [ctx.enter_context(nc.psum_tensor(f"x3p{j}", [P, S], f32)) for j in range(2)]
        dp = [ctx.enter_context(nc.psum_tensor(f"dp{i}", [P, 512], f32)) for i in range(4)]

        up_in = [sem(f"up_in{j}") for j in range(2)]
        dn_in = [sem(f"dn_in{j}") for j in range(2)]
        up_hi_done = [sem(f"up_hi_done{j}") for j in range(2)]
        dn_hi_done = [sem(f"dn_hi_done{j}") for j in range(2)]
        up_ready = [sem(f"up_ready{j}") for j in range(2)]
        dn_ready = [sem(f"dn_ready{j}") for j in range(2)]
        xt_in, xt_hi_done, xt_ready = sem("xt_in"), sem("xt_hi_done"), sem("xt_ready")
        rw_in, mask_a_in, mask_g_in, acc_in = sem("rw_in"), sem("mask_a_in"), sem("mask_g_in"), sem("acc_in")
        dp_ready, dp_free = sem("dp_ready"), sem("dp_free")
        ah_done, al_done = sem("ah_done"), sem("al_done")
        am0, am1 = sem("am0"), sem("am1")
        x1a, x3a, x1b, x3b = sem("x1a"), sem("x3a"), sem("x1b"), sem("x3b")
        silu0, silu1 = sem("silu0"), sem("silu1")
        p_done, q_done, s_done = sem("p_done"), sem("q_done"), sem("s_done")
        ph, sh, sl = sem("ph"), sem("sh"), sem("sl")
        g_done, gh, gl = sem("g_done"), sem("gh"), sem("gl")
        g_zero, y_out = sem("g_zero"), sem("y_out")
        gate, g_prod = sem("gate"), sem("g_prod")

        block = ctx.enter_context(nc.Block())

        DPB = 8 * GROUPS + 4

        def dp_base(b, g, last=False):
            late = isinstance(g, int) and g == GROUPS - 1 and not last
            return b * DPB + g * 8 + (8 if late else 4)

        def blocks(eng, body):
            with eng.Fori(0, B - 1) as b:
                body(b, False)
            body(B - 1, True)

        def pairs_of_chunks(eng, group, b, last):
            group(b, 0, last)
            with eng.Fori(1, GROUPS - 1) as g:
                group(b, g, last)
            group(b, GROUPS - 1, last)

        @block.sync
        def _(sp):
            def val(x):
                return x if isinstance(x, int) else sp.snap(x)

            def load(sem_free, need, dst, src, sem_in):
                need = val(need)
                sp.wait_ge(sem_free, need)
                sp.dma_start(dst, src).then_inc(sem_in, 16)

            def load_masks(dst, which, b, sem_in):
                for s, m in enumerate(which):
                    for e in range(E):
                        a, r0 = e // (P // R), (e % (P // R)) * R
                        sp.dma_start(dst[r0:r0 + R, s, a, :], sel_scr[b, m * E + e, :].partition_broadcast(R))\
                          .then_inc(sem_in, 16)

            def load_rw(b):
                for s in range(2):
                    sp.dma_start(rw[:, s, :], sel_scr[b, 3 * E + s, :].partition_broadcast(P)).then_inc(rw_in, 16)

            def group(b, g):
                q1 = val(b * GROUPS + g + 1)
                load(up_ready[1], q1, up_raw[1][:, :], w_scr[val(2 * g + 1), :, 0:UPC], up_in[1])
                for j in range(2):
                    load(dn_ready[j], q1, dn_raw[j][:, :], w_scr[val(2 * g + j), :, UPC:WCOLS], dn_in[j])
                load(up_ready[0], q1, up_raw[0][:, :], w_scr[val(2 * g + 2), :, 0:UPC], up_in[0])

            def body(b, last):
                group(b, 0)
                need = val(AC * b + 1)
                sp.wait_ge(gl, need)
                load_masks(mask_g, (1, 2), b, mask_g_in)
                load(y_out, 16 * b + 16, acc[:, :, :], x1_scr[b, :, :, :], acc_in)
                if not last:
                    load(xt_ready, KC * b + (KC + 1), xt_raw[:, :, :], xt_scr[val(b + 1), :, :, :], xt_in)
                    need0, need1 = val(2 * AC * b + 2 * AC), val(2 * AC * b + (2 * AC + 1))
                    nxt = val(b + 1)
                    sp.wait_ge(am0, need0)
                    sp.wait_ge(am1, need1)
                    load_masks(mask_a, (0, 2), nxt, mask_a_in)
                with sp.Fori(1, GROUPS) as g:
                    group(b, g)
                if not last:
                    nxt = val(b + 1)
                    need = val(FC * b + (FC + 2))
                    sp.wait_ge(q_done, need)
                    load_rw(nxt)

            sp.dma_start(xt_raw[:, :, :], xt_scr[0, :, :, :]).then_inc(xt_in, 16)
            sp.dma_start(up_raw[0][:, :], w_scr[0, :, 0:UPC]).then_inc(up_in[0], 16)
            load_masks(mask_a, (0, 2), 0, mask_a_in)
            load_rw(0)
            blocks(sp, body)

        @block.gpsimd
        def _(pool):
            def up_split(j, n):
                pool.wait_ge(up_hi_done[j], n)
                pool.tensor_tensor(up_lo[j][:, :], up_raw[j][:, :], up_hi[j][:, :].bitcast(f32), ALU.subtract)\
                    .then_inc(up_ready[j], 1)

            def dn_split(j, n):
                pool.wait_ge(dn_hi_done[j], n)
                pool.tensor_tensor(dn_lo[j][:, :], dn_raw[j][:, :], dn_hi[j][:, :].bitcast(f32), ALU.subtract)\
                    .then_inc(dn_ready[j], 1)

            def masked(b):
                pool.wait_ge(mask_a_in, 32 * E * (b + 1))
                for t in range(2 * AC):
                    m, a = t // AC, t % AC
                    pool.wait_ge(al_done, b * 2 * AC + (t + 1))
                    for dst, src in ((am_hi, gate0), (am_lo, gate1)):
                        ins = pool.tensor_tensor(dst[:, m, 1, a, :], src[t % 2][:, :], mask_a[:, 1, a, :], ALU.mult)
                    ins.then_inc(am1, 1)

            def body(b, last):
                with pool.Fori(0, GROUPS) as g:
                    q = b * GROUPS + g
                    up_split(1, q + 1)
                    up_split(0, q + 2)
                    dn_split(0, q + 1)
                    dn_split(1, q + 1)
                if not last:
                    masked(b + 1)

            up_split(0, 1)
            masked(0)
            blocks(pool, body)

        @block.scalar
        def _(act):
            def up_split(j, n):
                act.wait_ge(up_in[j], 16 * n)
                act.activation(up_hi[j][:, :], up_raw[j][:, :], ACT.Copy).then_inc(up_hi_done[j], 1)

            def dn_split(j, n):
                act.wait_ge(dn_in[j], 16 * n)
                act.activation(dn_hi[j][:, :], dn_raw[j][:, :], ACT.Copy).then_inc(dn_hi_done[j], 1)

            def xt_split(b):
                act.wait_ge(xt_in, 16 * (b + 1))
                for k in range(KC):
                    act.activation(xt_hi[:, k, :], xt_raw[:, k, :], ACT.Copy).then_inc(xt_hi_done, 1)

            def a_split(b, at):
                for t in range(2 * AC):
                    act.wait_ge(dp_ready, at + (t + 1))
                    if t >= 2:
                        act.wait_ge(am0, b * 2 * AC + (t - 1))
                        act.wait_ge(am1, b * 2 * AC + t)
                    act.activation(gate0[t % 2][:, :].bitcast(f32r), dp[t][:, :], ACT.Copy).then_inc(ah_done, 1)

            def group(b, g, last):
                q = b * GROUPS + g
                n = q * 2
                final = isinstance(g, int) and g == GROUPS - 1
                for j in range(2):
                    act.wait_ge(x1a, n + (j + 1))
                    act.activation(gate0[j][:, :], x1p[j][:, :], ACT.Silu).then_inc(silu0, 1)
                    if j == 0:
                        up_split(1, q + 1)
                    elif final and not last:
                        act.wait_ge(x3a, n + 2)
                        xt_split(b + 1)
                    act.wait_ge(x1b, n + (j + 1))
                    act.activation(gate1[j][:, :], x1p[j][:, :], ACT.Silu).then_inc(silu1, 1)
                    if j == 0:
                        act.wait_ge(dp_ready, b * DPB + g * 8 + 4)
                    act.wait_ge(p_done, n + (j + 1))
                    act.activation(p_hi[j][:, :], pq[j][:, :], ACT.Copy).then_inc(ph, 1)
                    act.wait_ge(s_done, n + (j + 1))
                    act.activation(s_hi[j][:, :], sq[j][:, :], ACT.Copy).then_inc(sh, 1)
                    if j == 0:
                        up_split(0, q + 2)
                        dn_split(0, q + 1)
                        dn_split(1, q + 1)

            def body(b, last):
                act.wait_ge(am1, 2 * AC * b + (2 * AC + 1))
                pairs_of_chunks(act, group, b, last)
                if not last:
                    a_split(b + 1, b * DPB + (DPB - 8))
                for a in range(AC):
                    act.wait_ge(g_done, b * AC + (a + 1))
                    act.activation(g_hi[a][:, :], g_acc[:, 0, a, :], ACT.Copy).then_inc(gh, 1)
                act.wait_ge(dp_free, dp_base(b, GROUPS - 1, last) + 12)
                act.dma_start(out[b, :, :].rearrange("(i p) h -> p i h", p=P), acc[:, :, :]).then_inc(y_out, 16)

            up_split(0, 1)
            xt_split(0)
            a_split(0, 0)
            blocks(act, body)
            act.wait_ge(y_out, 16 * B + 16)

        @block.vector
        def _(v):
            for x, (s, n) in enumerate(((dp_free, 4), (silu1, 2), (q_done, 2), (up_ready[1], 1), (dn_ready[0], 1),
                                        (dn_ready[1], 1), (gl, 1), (xt_ready, 1), (am1, 1), (y_out, 16))):
                v.memset(credit[:, x:x + 1], 0.0).then_inc(s, n)

            def zero_g():
                v.memset(g_acc[:, :, :, :], 0.0).then_inc(g_zero, 1)

            def xt_split(b):
                for k in range(KC):
                    v.wait_ge(xt_hi_done, b * KC + (k + 1))
                    v.tensor_tensor(xt_lo[:, k, :], xt_raw[:, k, :], xt_hi[:, k, :].bitcast(f32), ALU.subtract)\
                     .then_inc(xt_ready, 1)

            def masked(b):
                v.wait_ge(mask_a_in, 32 * E * (b + 1))
                for t in range(2 * AC):
                    m, a = t // AC, t % AC
                    v.wait_ge(ah_done, b * 2 * AC + (t + 1))
                    v.tensor_tensor(gate1[t % 2][:, :].bitcast(f32r), dp[t][:, :], gate0[t % 2][:, :], ALU.subtract)\
                     .then_inc(dp_free, 1)
                    v.tensor_tensor(am_hi[:, m, 0, a, :], gate0[t % 2][:, :], mask_a[:, 0, a, :], ALU.mult)\
                     .then_inc(al_done, 1)
                    v.wait_ge(al_done, b * 2 * AC + (t + 1))
                    v.tensor_tensor(am_lo[:, m, 0, a, :], gate1[t % 2][:, :], mask_a[:, 0, a, :], ALU.mult)\
                     .then_inc(am0, 1)

            def g_adds(at):
                for t in range(2 * AC):
                    v.wait_ge(dp_ready, at + (t + 1))
                    to = g_acc[:, t // AC, t % AC, :]
                    v.tensor_tensor(to, dp[t][:, :], to, ALU.add).then_inc(dp_free, 1)

            def out_adds(at):
                for i in range(TT):
                    v.wait_ge(dp_ready, at + (2 * AC + i + 1))
                    v.tensor_tensor(acc[:, i, :], dp[i][:, :], acc[:, i, :], ALU.add).then_inc(dp_free, 1)

            def group(b, g, last):
                n = b * FC + g * 2
                final = isinstance(g, int) and g == GROUPS - 1
                for j in range(2):
                    v.wait_ge(silu0, n + (j + 1))
                    v.tensor_tensor(gate0[j][:, :], gate0[j][:, :], rw[:, 0, :], ALU.mult).then_inc(gate, 1)
                    v.wait_ge(gate, n * 2 + (2 * j + 1))
                    v.wait_ge(x3a, n + (j + 1))
                    v.tensor_tensor(pq[j][:, :], x3p[j][:, :], gate0[j][:, :], ALU.mult).then_inc(p_done, 1)
                    if j == 0 and not (isinstance(g, int) and g == 0):
                        v.wait_ge(g_zero, b + 1)
                        v.wait_ge(acc_in, 16 * (b + 1))
                        g_adds(b * DPB + g * 8 - 4)
                        out_adds(b * DPB + g * 8 - 4)
                    if j == 1 and final and not last:
                        xt_split(b + 1)
                    v.wait_ge(silu1, n + (j + 3))
                    v.tensor_tensor(gate1[j][:, :], gate1[j][:, :], rw[:, 1, :], ALU.mult).then_inc(gate, 1)
                    v.wait_ge(gate, n * 2 + (2 * j + 2))
                    v.wait_ge(x3b, n + (j + 1))
                    v.tensor_tensor(sq[j][:, :], x3p[j][:, :], gate1[j][:, :], ALU.mult).then_inc(q_done, 1)
                    v.wait_ge(q_done, n + (j + 3))
                    v.tensor_tensor(sq[j][:, :], sq[j][:, :], pq[j][:, :], ALU.add).then_inc(s_done, 1)
                    v.wait_ge(ph, n + (j + 1))
                    v.tensor_tensor(p_lo[j][:, :], pq[j][:, :], p_hi[j][:, :].bitcast(f32), ALU.subtract)
                    v.wait_ge(sh, n + (j + 1))
                    v.tensor_tensor(s_lo[j][:, :], sq[j][:, :], s_hi[j][:, :].bitcast(f32), ALU.subtract)\
                     .then_inc(sl, 1)

            def body(b, last):
                v.wait_ge(rw_in, 32 * (b + 1))
                pairs_of_chunks(v, group, b, last)
                if not last:
                    masked(b + 1)
                at = dp_base(b, GROUPS - 1, last)
                g_adds(at)
                v.wait_ge(mask_g_in, 32 * E * (b + 1))
                v.wait_ge(dp_free, at + 8)
                for a in range(AC):
                    v.tensor_tensor(g_acc[:, 0, a, :], g_acc[:, 0, a, :], mask_g[:, 0, a, :], ALU.mult)
                    v.tensor_tensor(g_acc[:, 1, a, :], g_acc[:, 1, a, :], mask_g[:, 1, a, :], ALU.mult)\
                     .then_inc(g_prod, 1)
                for a in range(AC):
                    v.wait_ge(g_prod, b * AC + (a + 1))
                    v.tensor_tensor(g_acc[:, 0, a, :], g_acc[:, 0, a, :], g_acc[:, 1, a, :], ALU.subtract)\
                     .then_inc(g_done, 1)
                for a in range(AC):
                    v.wait_ge(gh, b * AC + (a + 1))
                    v.tensor_tensor(g_lo[a][:, :], g_acc[:, 0, a, :], g_hi[a][:, :].bitcast(f32), ALU.subtract)\
                     .then_inc(gl, 1)
                out_adds(at)
                if not last:
                    v.wait_ge(gl, AC * b + (AC + 1))
                    zero_g()

            zero_g()
            xt_split(0)
            masked(0)
            blocks(v, body)

        @block.tensor
        def _(pe):
            def product(dst, operands, start, stop):
                for x, (lh, ll, rh, rl) in enumerate(operands):
                    for y, (lhs, rhs) in enumerate(((lh, rh), (lh, rl), (ll, rh))):
                        mm = pe.matmul(dst, lhs, rhs, start=start and x == 0 and y == 0,
                                       stop=stop and x == len(operands) - 1 and y == 2, skip_group_check=True)
                return mm

            def base(j, m):
                at = m * KC * P
                return [(up_hi[j][:, at + k * P:at + (k + 1) * P], up_lo[j][:, at + k * P:at + (k + 1) * P],
                         xt_hi[:, k, :], xt_lo[:, k, :]) for k in range(KC)]

            def lora(j, m, s):
                at = LORA + m * AC * P
                return [(up_hi[j][:, at + a * P:at + (a + 1) * P], up_lo[j][:, at + a * P:at + (a + 1) * P],
                         am_hi[:, m, s, a, :], am_lo[:, m, s, a, :]) for a in range(AC)]

            def a_tiles(b, at):
                for t in range(2 * AC):
                    m, a = t // AC, t % AC
                    pe.wait_ge(dp_free, at + (t + 1))
                    c = slice(a * P, (a + 1) * P)
                    for k in range(KC):
                        if t == 0:
                            pe.wait_ge(xt_ready, b * KC + (k + 2))
                        mm = product(dp[t][:, :], [(A13h[:, m, k, c], A13l[:, m, k, c], xt_hi[:, k, :],
                                                    xt_lo[:, k, :])], k == 0, k == KC - 1)
                    mm.then_inc(dp_ready, 1)

            def down(b, g, at, finish=False):
                q = b * GROUPS + g
                for j in range(2):
                    pe.wait_ge(dn_ready[j], q + 2)
                pe.wait_ge(sl, q * 2 + 2)
                for t in range(2 * AC):
                    pe.wait_ge(dp_free, at + (t + 1))
                    c = slice(H + (t % AC) * P, H + (t % AC + 1) * P)
                    hi, lo = (s_hi, s_lo) if t < AC else (p_hi, p_lo)
                    product(dp[t][:, :], [(dn_hi[j][:, c], dn_lo[j][:, c], hi[j][:, :], lo[j][:, :])
                                          for j in range(2)], True, True).then_inc(dp_ready, 1)
                for i in range(TT):
                    pe.wait_ge(dp_free, at + (2 * AC + i + 1))
                    c = slice(i * P, (i + 1) * P)
                    mm = product(dp[i][:, :], [(s_hi[j][:, c], s_lo[j][:, c], dn_hi[j][:, 0:H], dn_lo[j][:, 0:H])
                                               for j in range(2)], True, not finish)
                    if not finish:
                        mm.then_inc(dp_ready, 1)
                if finish:
                    pe.wait_ge(gl, AC * b + (AC + 1))
                    for i in range(TT):
                        c = slice(i * P, (i + 1) * P)
                        product(dp[i][:, :], [(g_hi[a][:, c], g_lo[a][:, c], B2h[:, a, :], B2l[:, a, :])
                                              for a in range(AC)], False, True).then_inc(dp_ready, 1)

            def group(b, g, last):
                q = b * GROUPS + g
                n = q * 2
                opening = isinstance(g, int) and g == 0
                for j in range(2):
                    pe.wait_ge(up_ready[j], q + (1 + j))
                    pe.wait_ge(silu1, n + (j + 1))
                    if opening and j == 0:
                        pe.wait_ge(am0, b * 2 * AC + 2 * AC)
                    product(x1p[j][:, :], base(j, 0) + lora(j, 0, 0), True, True).then_inc(x1a, 1)
                    pe.wait_ge(q_done, n + (j + 1))
                    product(x3p[j][:, :], base(j, 1) + lora(j, 1, 0), True, True).then_inc(x3a, 1)
                    if j == 0 and not opening:
                        down(b, g - 1, b * DPB + g * 8 - 4)
                    pe.wait_ge(silu0, n + (j + 1))
                    if opening and j == 0:
                        pe.wait_ge(am1, b * 2 * AC + (2 * AC + 1))
                    product(x1p[j][:, :], lora(j, 0, 1), False, True).then_inc(x1b, 1)
                    pe.wait_ge(p_done, n + (j + 1))
                    product(x3p[j][:, :], lora(j, 1, 1), False, True).then_inc(x3b, 1)

            def body(b, last):
                pairs_of_chunks(pe, group, b, last)
                if not last:
                    a_tiles(b + 1, b * DPB + (DPB - 8))
                down(b, GROUPS - 1, dp_base(b, GROUPS - 1, last), finish=True)

            a_tiles(0, 0)
            blocks(pe, body)


def build(nc, io, out):
    def dram(name, shape):
        return nc.dram_tensor(name, shape, f32, kind="Internal").ap()

    scratch = (dram("w_scr", (FC + 1, P, WCOLS)), dram("x1_scr", (B, P, TT, H)),
               dram("xt_scr", (B, P, KC, S)), dram("sel_scr", (B, SELR, S)))
    with (nc.sbuf_tensor("A13h", [P, 2, KC, ER], f32r) as A13h, nc.sbuf_tensor("A13l", [P, 2, KC, ER], f32r) as A13l,
          nc.sbuf_tensor("B2h", [P, AC, H], f32r) as B2h, nc.sbuf_tensor("B2l", [P, AC, H], f32r) as B2l):
        keep = (A13h, A13l, B2h, B2l)
        build_front(nc, io, scratch, keep)
        build_ffn(nc, out, scratch, keep)


_INS = {"x": "x", "ctx_2048": "ctx", "itok_Sx4_0_63": "tok", "L0_xattn_desc_router": "desc", "L0_xattn_W_q": "W_q",
        "L0_xattn_b_q": "b_q", "L0_ffn_Wg": "Wg", "L0_ffn_W1": "W1", "L0_ffn_W2": "W2", "L0_ffn_W3": "W3",
        "L0_ffn_A1": "A1", "L0_ffn_B1": "B1", "L0_ffn_A2": "A2", "L0_ffn_B2": "B2", "L0_ffn_A3": "A3",
        "L0_ffn_B3": "B3"}


def kernel(**inputs):
    import numpy as _np
    import concourse.bacc as _bacc
    from concourse import mybir as _mybir
    from concourse.bass_utils import run_bass_kernel_spmd as _run

    nc = _bacc.Bacc("TRN2", target_bir_lowering=False, num_devices=1)
    arrays, io = {}, {}
    for name, short in _INS.items():
        a = _np.ascontiguousarray(inputs[name])
        arrays[f"in_{name}"] = a
        io[short] = nc.dram_tensor(f"in_{name}", a.shape, _mybir.dt.from_np(a.dtype), kind="ExternalInput").ap()
    out = nc.dram_tensor("out_0", (B, S, H), _mybir.dt.float32, kind="ExternalOutput").ap()
    build(nc, io, out)
    r = _run(nc, [arrays], core_ids=[0])
    return r.results[0]["out_0"]
```

```python
import concourse.bass as bass
from concourse import mybir
from contextlib import ExitStack

P = 128
B, S, H, F = 8, 512, 512, 1792
N, TOK = 64, 4
E, R = 8, 32
ER = E * R
KC = H // P
TT = S // P
FC = F // P
AC = ER // P
GROUPS = FC // 2
UPC = 2 * KC * P + 2 * AC * P
DNC = H + ER
WCOLS = UPC + DNC
LORA = 2 * KC * P
SELR = 32
EPS = 1e-5
FAR = 3.0e38
SCALE = float(H) ** -0.5

f32 = mybir.dt.float32
f32r = mybir.dt.float32r
i32 = mybir.dt.int32
u32 = mybir.dt.uint32
ALU = mybir.AluOpType
ACT = mybir.ActivationFunctionType


def build_front(nc, io, scratch, keep):
    w_scr, x1_scr, xt_scr, sel_scr = scratch
    A13h, A13l, B2h, B2l, xt_raw, xt_hi, xt_lo = keep
    with ExitStack() as ctx:
        def sb(name, shape, dt=f32):
            return ctx.enter_context(nc.sbuf_tensor(name, shape, dt))

        def sem(name):
            return ctx.enter_context(nc.semaphore(name))

        ident = sb("ident", [P, P])
        iota_set = sb("iota_set", [P, N])
        iota_exp = sb("iota_exp", [P, E])
        ones_row = sb("ones_row", [1, P])
        a_nat = sb("a_nat", [P, 2, AC, H])
        b2_nat = sb("b2_nat", [P, KC, E, R])
        wg_nat = sb("wg_nat", [E, H])
        desc_nat = sb("desc_nat", [N, H])
        wq_nat = sb("wq_nat", [P, KC, H])
        bq_nat = sb("bq_nat", [KC, P])
        bq_col = sb("bq_col", [P, KC])
        tok_i = sb("tok_i", [P, TT, TOK], i32)
        tok_f = sb("tok_f", [P, TT, TOK])
        member = sb("member", [P, TT, N])
        hit = sb("hit", [P, TT, N])
        penalty = sb("penalty", [P, TT, N])
        desc_t = sb("desc_t", [P, KC, N])
        wg_t = sb("wg_t", [P, KC, E])
        score_w = sb("score_w", [P, KC, N])
        score_b = sb("score_b", [1, N])

        w_nat = [sb(f"w_nat{j}", [P, WCOLS]) for j in range(2)]
        w_t = [sb(f"w_t{j}", [P, WCOLS]) for j in range(2)]

        x_in = sb("x_in", [P, 2, TT, H])
        ctx_in = sb("ctx_in", [N, H])
        x1 = sb("x1", [P, TT, H])
        xna, xnb = sb("xna", [P, TT, H]), sb("xnb", [P, TT, H])
        xta, xtb = sb("xta", [P, KC, S]), sb("xtb", [P, KC, S])
        norm_a = [sb(f"norm_a{n}", [P, TT, w]) for n, w in enumerate((6, 2, 1, 1, 1, 1))]
        norm_b = [sb(f"norm_b{n}", [P, TT, w]) for n, w in enumerate((6, 2, 1, 1, 1, 1))]
        best_a = [sb(f"best_a{n}", [P, TT, w]) for n, w in enumerate((8, 8, 1, 1, 1, 2))]
        best_b = [sb(f"best_b{n}", [P, TT, w]) for n, w in enumerate((8, 8, 1, 1, 1, 2))]
        bidx_a, bidx_b = sb("bidx_a", [P, TT, 8], u32), sb("bidx_b", [P, TT, 8], u32)
        sc = sb("sc", [P, TT, N])
        lg = sb("lg", [P, TT, E])
        oh = sb("oh", [P, 2, TT, N])
        wd = sb("wd", [P, TT, P])
        wd_t = sb("wd_t", [N, S])
        sel = sb("sel", [P, TT, SELR])
        sel_t = sb("sel_t", [SELR, S])
        credit = sb("credit_front", [P, 8])
        carrier_cells = sb("carrier_cells", [P, 4])

        def bank(name):
            return ctx.enter_context(nc.psum_tensor(name, [P, 512], f32))

        pt = [bank(f"pt{i}") for i in range(5)]
        p_sc, p_lg, p_mix = bank("p_sc"), bank("p_lg"), bank("p_mix")

        consts = sem("consts")
        att_in, small_in = sem("att_in"), sem("small_in")
        desc_ready, desc_done = sem("desc_ready"), sem("desc_done")
        small_t = sem("small_t")
        small_hi = sem("small_hi")
        small_lo = sem("small_lo")
        sw_ready = sem("sw_ready")
        sw_done = sem("sw_done")
        nat_in = [sem(f"nat_in{j}") for j in range(2)]
        wt_ready = sem("wt_ready")
        wt_done = sem("wt_done")
        ws_out = [sem(f"ws_out{j}") for j in range(2)]
        ws_wrap = sem("ws_wrap")
        x_loaded, ctx_loaded = sem("x_loaded"), sem("ctx_loaded")
        x1_out, xt_out, sel_out = sem("x1_out"), sem("xt_out"), sem("sel_out")
        order = sem("order")
        norm_order_a, norm_order_b = sem("norm_order_a"), sem("norm_order_b")
        order_a, order_b = sem("order_a"), sem("order_b")
        ve_a, ve_b = sem("ve_a"), sem("ve_b")
        sd_a, sd_b = sem("sd_a"), sem("sd_b")
        xn_a, xn_b = sem("xn_a"), sem("xn_b")
        xt_ready_a, xt_ready_b = sem("xt_ready_a"), sem("xt_ready_b")
        xt_done_a, xt_done_b = sem("xt_done_a"), sem("xt_done_b")
        sc_ready, lg_ready = sem("sc_ready"), sem("lg_ready")
        gap_a, gap_b = sem("gap_a"), sem("gap_b")
        eg_a, eg_b = sem("eg_a"), sem("eg_b")
        wd_done, sel_done = sem("wd_done"), sem("sel_done")
        wdt_ready, selt_ready = sem("wdt_ready"), sem("selt_ready")
        wdt_done, selt_done = sem("wdt_done"), sem("selt_done")
        first_in, first_hi, first_lo = sem("first_in"), sem("first_hi"), sem("first_lo")
        mix_ready = sem("mix_ready")
        x1_done = sem("x1_done")

        block = ctx.enter_context(nc.Block())

        NAT = [("W1", 0, H), ("W3", H, H), ("B1", 2 * H, ER), ("B3", 2 * H + ER, ER),
               ("W2", 2 * H + 2 * ER, H), ("A2", 3 * H + 2 * ER, ER)]
        NATS = 16 * len(NAT)

        def nat_loads(sp, j, at):
            w = w_nat[j]
            rows = bass.ds(at, P)
            for name, col, width in NAT:
                dst = w[:, col:col + width]
                if name in ("W1", "W3"):
                    src = io[name][rows, :]
                elif name in ("B1", "B3"):
                    src = io[name][:, rows, :].rearrange("e f r -> f e r")
                    dst = dst.rearrange("p (e r) -> p e r", e=E)
                elif name == "W2":
                    src = io[name][:, rows].rearrange("(k p) f -> p k f", p=P)
                    dst = dst.rearrange("p (k f) -> p k f", k=KC)
                else:
                    src = io[name].rearrange("e r f -> (e r) f")[:, rows].rearrange("(a p) f -> p a f", p=P)
                    dst = dst.rearrange("p (a f) -> p a f", a=AC)
                sp.dma_start(dst, src).then_inc(nat_in[j], 16)

        @block.sync
        def _(sp):
            for dst, src in (
                (desc_nat[:, :], io["desc"]),
                (wq_nat[:, :, :], io["W_q"].rearrange("(k p) d -> p k d", p=P)),
                (bq_nat[:, :], io["b_q"].rearrange("(k p) -> k p", p=P)),
                (tok_i[:, :, :], io["tok"].rearrange("(i p) k -> p i k", p=P)),
            ):
                sp.dma_start(dst, src).then_inc(att_in, 16)
            for dst, src in (
                (a_nat[:, 0, :, :], io["A1"].rearrange("e r h -> (e r) h").rearrange("(a p) h -> p a h", p=P)),
                (a_nat[:, 1, :, :], io["A3"].rearrange("e r h -> (e r) h").rearrange("(a p) h -> p a h", p=P)),
                (b2_nat[:, 0, :, :], io["B2"][:, 0:P, :].rearrange("e p r -> p e r")),
                (b2_nat[:, 1, :, :], io["B2"][:, P:2 * P, :].rearrange("e p r -> p e r")),
                (b2_nat[:, 2, :, :], io["B2"][:, 2 * P:3 * P, :].rearrange("e p r -> p e r")),
                (b2_nat[:, 3, :, :], io["B2"][:, 3 * P:4 * P, :].rearrange("e p r -> p e r")),
                (wg_nat[:, :], io["Wg"]),
            ):
                sp.dma_start(dst, src).then_inc(small_in, 16)
            for j in range(2):
                nat_loads(sp, j, j * P)

            def val(x):
                return x if isinstance(x, int) else sp.snap(x)

            def store_rows(b):
                need, dst = val(TT * b + TT), xt_scr[val(b), :, :, :]
                sp.wait_ge(xt_done_b, need)
                sp.dma_start(dst, xtb[:, :, :]).then_inc(xt_out, 16)

            def store_table(b):
                need, dst = val(b + 2), sel_scr[val(b), :, :]
                sp.wait_ge(selt_done, need)
                sp.dma_start(dst, sel_t[:, :]).then_inc(sel_out, 16)

            with sp.Fori(0, GROUPS - 1) as i:
                store_rows(i)
                for j in range(2):
                    at, need = val(2 * P * i + (2 + j) * P), val(10 * i + (5 * j + 5))
                    sp.wait_ge(wt_ready, need)
                    nat_loads(sp, j, at)
                store_table(i)
            sp.wait_ge(xt_out, 16 + 16)
            sp.dma_start(xt_raw[:, :, :], xt_scr[0, :, :, :]).then_inc(first_in, 16)
            store_rows(GROUPS - 1)
            sp.wait_ge(ws_out[0], 16 * GROUPS + 16)
            sp.dma_start(w_scr[FC, :, :], w_scr[0, :, :]).then_inc(ws_wrap, 16)
            store_table(GROUPS - 1)
            store_rows(B - 1)
            store_table(B - 1)

        @block.gpsimd
        def _(pool):
            xr = io["x"].rearrange("b (i p) h -> b p i h", p=P)
            pool.dma_start(x_in[:, 0, :, :], xr[0, :, :, :]).then_inc(x_loaded, 16)
            pool.memset(ident[:, :], 0.0).then_inc(consts, 1)
            pool.wait_ge(consts, 1)
            pool.affine_select(out=ident[:, :], in_=ident[:, :], compare_op=ALU.not_equal, fill=1.0,
                               base=0, pattern=[[-1, P]], channel_multiplier=1).then_inc(consts, 1)
            pool.memset(ones_row[:, :], 1.0).then_inc(consts, 1)
            pool.memset(sel[:, :, :], 0.0).then_inc(consts, 1)
            pool.memset(wd[:, :, :], 0.0).then_inc(consts, 1)
            pool.iota(iota_set[:, :], pattern=[[1, N]], base=0, channel_multiplier=0,
                      allow_small_or_imprecise_dtypes=True).then_inc(consts, 1)
            pool.iota(iota_exp[:, :], pattern=[[1, E]], base=0, channel_multiplier=0,
                      allow_small_or_imprecise_dtypes=True).then_inc(consts, 1)
            pool.dma_start(ctx_in[:, :], io["ctx"][0, :, :]).then_inc(ctx_loaded, 16)
            pool.wait_ge(x_loaded, 16)
            pool.dma_start(x_in[:, 1, :, :], xr[1, :, :, :]).then_inc(x_loaded, 16)

            def val(x):
                return x if isinstance(x, int) else pool.snap(x)

            def after_a(b, ctx_next, x_next):
                need, need_x = val(TT * b + TT), val(16 * b + 32)
                slot, nxt, nxt2 = val(b & 1), val(b + 1), val(b + 2)
                pool.wait_ge(x1_done, need)
                pool.dma_start(x1_scr[b, :, :, :], x1[:, :, :]).then_inc(x1_out, 16)
                if ctx_next:
                    pool.dma_start(ctx_in[:, :], io["ctx"][nxt, :, :]).then_inc(ctx_loaded, 16)
                if x_next:
                    pool.wait_ge(x_loaded, need_x)
                    pool.dma_start(x_in[:, slot, :, :], xr[nxt2, :, :, :]).then_inc(x_loaded, 16)

            after_a(0, True, True)
            with pool.Fori(1, B - 2) as b:
                after_a(b, True, True)
            after_a(B - 2, True, False)
            after_a(B - 1, False, False)
            for s, n in ((x1_out, B), (xt_out, B + 1), (sel_out, B + 1), (ws_wrap, 1), (ws_out[0], GROUPS + 1),
                         (ws_out[1], GROUPS + 1)):
                pool.wait_ge(s, 16 * n)

        @block.tensor
        def _(pe):
            pe.wait_ge(consts, 7)
            pe.wait_ge(att_in, 16 * 4)
            for k in range(KC):
                pe.transpose(pt[4][:, k * N:(k + 1) * N], desc_nat[:, k * P:(k + 1) * P], ident[0:N, 0:N])
            pe.transpose(pt[4][:, KC * N:KC * N + KC], bq_nat[:, :], ident[0:KC, 0:KC]).then_inc(desc_ready, 1)
            pe.wait_ge(desc_done, 1)
            for d in range(KC):
                for k in range(KC):
                    pe.matmul(p_sc[:, d * N:(d + 1) * N], wq_nat[:, k, d * P:(d + 1) * P], desc_t[:, k, :],
                              start=(k == 0), stop=(k == KC - 1))
            for k in range(KC):
                mm = pe.matmul(p_sc[0:1, KC * N:KC * N + N], bq_col[:, k:k + 1], desc_t[:, k, :],
                               start=(k == 0), stop=(k == KC - 1))
            mm.then_inc(sw_ready, 1)
            pe.wait_ge(sw_done, 1)

            def small_a():
                pe.wait_ge(small_in, 16 * 7)
                for bk in range(4):
                    m, half = bk // 2, bk % 2
                    for kk in range(2):
                        for a in range(AC):
                            k = 2 * half + kk
                            mm = pe.transpose(pt[bk][:, kk * ER + a * P:kk * ER + (a + 1) * P],
                                              a_nat[:, m, a, k * P:(k + 1) * P], ident[:, :])
                    mm.then_inc(small_t, 1)

            def small_b():
                for a in range(AC):
                    pe.wait_ge(small_lo, a + 1)
                    for k in range(KC):
                        mm = pe.transpose(pt[a][:, k * P:(k + 1) * P],
                                          b2_nat[:, k, 4 * a:4 * a + 4, :].rearrange("p e r -> p (e r)"), ident[:, :])
                    mm.then_inc(small_t, 1)
                pe.wait_ge(small_lo, 3)
                for k in range(KC):
                    mm = pe.transpose(pt[2][:, k * E:(k + 1) * E], wg_nat[:, k * P:(k + 1) * P], ident[0:E, 0:E])
                mm.then_inc(small_t, 1)

            def chunk(i, j):
                pe.wait_ge(nat_in[j], NATS * i + NATS)
                for t in range(5):
                    if j:
                        pe.wait_ge(wt_done, 10 * i + (t + 1))
                    elif t < TT:
                        pe.wait_ge(xt_done_b, TT * i + (t + 1))
                    else:
                        pe.wait_ge(x1_done, TT * i + TT)
                    lo, hi = 512 * t, min(512 * (t + 1), WCOLS)
                    for q in range(lo, hi, P):
                        mm = pe.transpose(pt[t][:, q - lo:q - lo + P], w_nat[j][:, q:q + P], ident[:, :])
                    mm.then_inc(wt_ready, 1)

            def rows_a(b):
                for i in range(TT):
                    pe.wait_ge(xn_a, TT * b + (i + 1))
                    for k in range(KC):
                        mm = pe.transpose(pt[i][:, k * P:(k + 1) * P], xna[:, i, k * P:(k + 1) * P], ident[:, :])
                    mm.then_inc(xt_ready_a, 1)

            def rows_b(b):
                for i in range(TT):
                    pe.wait_ge(xn_b, TT * b + (i + 1))
                    for k in range(KC):
                        mm = pe.transpose(pt[i][:, k * P:(k + 1) * P], xnb[:, i, k * P:(k + 1) * P], ident[:, :])
                    mm.then_inc(xt_ready_b, 1)

            def scores(b):
                for i in range(TT):
                    pe.wait_ge(xt_done_a, TT * b + (i + 1))
                    for k in range(KC):
                        pe.matmul(p_sc[:, i * N:(i + 1) * N], xta[:, k, i * P:(i + 1) * P], score_w[:, k, :],
                                  start=(k == 0), stop=False)
                    mm = pe.matmul(p_sc[:, i * N:(i + 1) * N], ones_row[:, :], score_b[:, :], start=False, stop=True)
                mm.then_inc(sc_ready, 1)

            def logits(b):
                pe.wait_ge(selt_done, b + 1)
                for i in range(TT):
                    pe.wait_ge(xt_done_b, TT * b + (i + 1))
                    for k in range(KC):
                        mm = pe.matmul(p_lg[:, i * E:(i + 1) * E], xtb[:, k, i * P:(i + 1) * P], wg_t[:, k, :],
                                       start=(k == 0), stop=(k == KC - 1))
                mm.then_inc(lg_ready, 1)

            def table(b):
                for i in range(TT):
                    mm = pe.transpose(p_lg[0:SELR, i * P:(i + 1) * P], sel[:, i, :], ident[:, :])
                mm.then_inc(selt_ready, 1)

            def weights(b):
                for i in range(TT):
                    mm = pe.transpose(p_sc[:, i * P:(i + 1) * P], wd[:, i, :], ident[:, :])
                mm.then_inc(wdt_ready, 1)

            def mixture(b, pair):
                pe.wait_ge(wdt_done, b + 1)
                pe.wait_ge(ctx_loaded, 16 * b + 16)
                for i in range(TT):
                    if i == 1 and pair:
                        pe.wait_ge(wt_done, 10 * b)
                    if i >= 2:
                        pe.wait_ge(x1_done, TT * b + (i - 1))
                    pe.matmul((p_mix, pt[4])[i % 2][:, :], wd_t[:, i * P:(i + 1) * P], ctx_in[:, :],
                              start=True, stop=True).then_inc(mix_ready, 1)

            rows_a(0)
            scores(0)
            small_a()
            pe.wait_ge(wd_done, 1)
            weights(0)
            mixture(0, False)
            small_b()
            pe.wait_ge(small_lo, 7)
            rows_a(1)
            scores(1)
            rows_b(0)
            logits(0)

            def turn(b, last):
                chunk(b - 1, 0)
                chunk(b - 1, 1)
                pe.wait_ge(wd_done, b + 1)
                weights(b)
                mixture(b, True)
                if not last:
                    rows_a(b + 1)
                    scores(b + 1)
                pe.wait_ge(sel_done, b)
                table(b - 1)
                rows_b(b)
                logits(b)

            with pe.Fori(1, B - 1) as b:
                turn(b, False)
            turn(B - 1, True)
            pe.wait_ge(sel_done, B)
            table(B - 1)

        @block.scalar
        def _(act):
            def small_hi_part(bk):
                act.wait_ge(small_t, bk + 1)
                if bk < 4:
                    dst = A13h[:, bk // 2, 2 * (bk % 2):2 * (bk % 2) + 2, :].rearrange("p k c -> p (k c)")
                else:
                    dst = B2h[:, bk - 4, :]
                act.activation(dst, pt[bk % 4][:, :], ACT.Copy).then_inc(small_hi, 1)

            def chunk(i, j):
                act.wait_ge(ws_out[j], 16 * i + 16)
                for t in range(5):
                    act.wait_ge(wt_ready, 10 * i + (5 * j + t + 1))
                    lo, hi = 512 * t, min(512 * (t + 1), WCOLS)
                    act.activation(w_t[j][:, lo:hi], pt[t][:, 0:hi - lo], ACT.Copy).then_inc(wt_done, 1)
                act.wait_ge(wt_done, 10 * i + (5 * j + 5))
                act.dma_start(w_scr[2 * i + j, :, :], w_t[j][:, :]).then_inc(ws_out[j], 16)

            def root(b, norm, ve, sd):
                act.wait_ge(ve, b + 1)
                act.activation(norm[3][:, :, 0], norm[2][:, :, 0], ACT.Sqrt).then_inc(sd, 1)

            def take(b, dst, ready, done):
                for i in range(TT):
                    act.wait_ge(ready, TT * b + (i + 1))
                    act.activation(dst[:, :, i * P:(i + 1) * P], pt[i][:, :].rearrange("p (k t) -> p k t", k=KC),
                                   ACT.Copy).then_inc(done, 1)

            def expo(b, best, gap, eg, scale):
                act.wait_ge(gap, b + 1)
                act.activation(best[3][:, :, 0], best[2][:, :, 0], ACT.Exp, scale=scale).then_inc(eg, 1)

            def take_table(b):
                act.wait_ge(sel_out, 16 * b + 16)
                act.wait_ge(selt_ready, b + 1)
                act.activation(sel_t[:, :], p_lg[0:SELR, :], ACT.Copy).then_inc(selt_done, 1)

            def take_weights(b):
                act.wait_ge(wdt_ready, b + 1)
                act.activation(wd_t[:, :], p_sc[0:N, :], ACT.Copy).then_inc(wdt_done, 1)

            def rows_in_b(b):
                act.wait_ge(xt_out, 16 * b + 16)
                take(b, xtb, xt_ready_b, xt_done_b)

            root(0, norm_a, ve_a, sd_a)
            take(0, xta, xt_ready_a, xt_done_a)
            expo(0, best_a, gap_a, eg_a, SCALE)
            for bk in range(4):
                small_hi_part(bk)
            take_weights(0)
            for bk in range(4, 6):
                small_hi_part(bk)
            root(1, norm_a, ve_a, sd_a)
            take(1, xta, xt_ready_a, xt_done_a)
            root(0, norm_b, ve_b, sd_b)
            rows_in_b(0)

            def turn(b, last):
                expo(b, best_a, gap_a, eg_a, SCALE)
                chunk(b - 1, 0)
                chunk(b - 1, 1)
                take_weights(b)
                expo(b - 1, best_b, gap_b, eg_b, 1.0)
                if not last:
                    root(b + 1, norm_a, ve_a, sd_a)
                    take(b + 1, xta, xt_ready_a, xt_done_a)
                root(b, norm_b, ve_b, sd_b)
                take_table(b - 1)
                rows_in_b(b)

            with act.Fori(1, B - 1) as b:
                turn(b, False)
            act.wait_ge(first_in, 16)
            for k in range(KC):
                act.activation(xt_hi[:, k, :], xt_raw[:, k, :], ACT.Copy).then_inc(first_hi, 1)
            turn(B - 1, True)
            expo(B - 1, best_b, gap_b, eg_b, 1.0)
            take_table(B - 1)

        @block.vector
        def _(v):
            for x, (s, n) in enumerate(((selt_done, 1), (ws_out[0], 16), (ws_out[1], 16), (xt_out, 16),
                                        (sel_out, 16))):
                v.memset(credit[:, x:x + 1], 0.0).then_inc(s, n)

            def counter(s, base):
                count = [0]

                def link(ins, carrier=None):
                    count[0] += 1
                    ins.then_inc(s, 1)
                    v.wait_ge(s, base + count[0])
                    if carrier is not None:
                        v.tensor_copy(carrier_cells[:, carrier:carrier + 1], credit[:, 0:1])
                return link, count

            def small_lo_part(bk):
                v.wait_ge(small_hi, bk + 1)
                if bk < 4:
                    at = (slice(None), bk // 2, slice(2 * (bk % 2), 2 * (bk % 2) + 2), slice(None))
                    h, lo = A13h[at].rearrange("p k c -> p (k c)"), A13l[at].rearrange("p k c -> p (k c)")
                else:
                    h, lo = B2h[:, bk - 4, :], B2l[:, bk - 4, :]
                v.tensor_tensor(lo, pt[bk % 4][:, :], h.bitcast(f32), ALU.subtract).then_inc(small_lo, 1)

            def allowed_sets():
                link, _c = counter(order, 0)
                v.wait_ge(consts, 7)
                v.wait_ge(att_in, 16 * 4)
                link(v.tensor_copy(tok_f[:, :, :], tok_i[:, :, :]))
                iota_b = iota_set[:, :].unsqueeze(1).to_broadcast([P, TT, N])
                for k in range(TOK):
                    tok_b = tok_f[:, :, k:k + 1].to_broadcast([P, TT, N])
                    link(v.tensor_tensor((hit if k else member)[:, :, :], iota_b, tok_b, ALU.is_equal))
                    if k:
                        link(v.tensor_tensor(member[:, :, :], member[:, :, :], hit[:, :, :], ALU.max))
                link(v.tensor_scalar(penalty[:, :, :], member[:, :, :], 1.0, FAR, ALU.subtract, ALU.mult))

            ORDER_N, ORDER_A, ORDER_B = 2 + 5, 1 + 6 + 1, 1 + 6

            def stats(b, src, norm, order_s, ve):
                bn, mv, vv = norm[0], norm[1], norm[2]
                link, _c = counter(order_s, ORDER_N * b)
                for i in range(TT):
                    ins = v.bn_stats(bn[:, i, :], src[:, i, :])
                link(ins, carrier=int(norm is norm_b))
                for i in range(TT):
                    ins = v.bn_aggr(mv[:, i, :], bn[:, i, :])
                link(ins)
                v.tensor_scalar(vv[:, :, 0], mv[:, :, 1], EPS, None, ALU.add).then_inc(ve, 1)

            def normalise(b, src, dst, norm, order_s, sd, xn):
                mv, vv, sdv, rs, nt = norm[1:]
                link, _c = counter(order_s, ORDER_N * b + 2)
                v.wait_ge(sd, b + 1)
                link(v.reciprocal(rs[:, :, 0], sdv[:, :, 0]))
                link(v.tensor_tensor(nt[:, :, 0], rs[:, :, 0], rs[:, :, 0], ALU.mult))
                link(v.tensor_tensor(nt[:, :, 0], nt[:, :, 0], vv[:, :, 0], ALU.mult))
                link(v.tensor_scalar(nt[:, :, 0], nt[:, :, 0], -0.5, 1.5, ALU.mult, ALU.add))
                link(v.tensor_tensor(rs[:, :, 0], rs[:, :, 0], nt[:, :, 0], ALU.mult))
                for i in range(TT):
                    v.tensor_scalar(dst[:, i, :], src[:, i, :], mv[:, i, 0:1], rs[:, i, 0:1],
                                    ALU.subtract, ALU.mult).then_inc(xn, 1)

            def two_best(b, vals, iota, width, best, bidx, order_s, per, at, gap, dst0, dst1):
                top, top_i, gp = best[0], best[1], best[2]
                link, count = counter(order_s, per * b + at)
                for i in range(TT):
                    ins = v.max(top[:, i, :], vals[:, i, :])
                link(ins)
                v.tensor_tensor(gp[:, :, 0], top[:, :, 1], top[:, :, 0], ALU.subtract).then_inc(gap, 1)
                for i in range(TT):
                    ins = v.max_index(bidx[:, i, :], top[:, i, :], vals[:, i, :])
                link(ins)
                link(v.tensor_copy(top_i[:, :, :], bidx[:, :, :]))
                it = iota[:, :].unsqueeze(1).to_broadcast([P, TT, width])
                v.tensor_tensor(dst0, it, top_i[:, :, 0:1].to_broadcast([P, TT, width]), ALU.is_equal)
                v.tensor_tensor(dst1, it, top_i[:, :, 1:2].to_broadcast([P, TT, width]), ALU.is_equal)
                return at + count[0]

            def softmax_two(b, best, order_s, per, at, eg):
                e, den, w = best[3], best[4], best[5]
                link, count = counter(order_s, per * b + at)
                v.wait_ge(eg, b + 1)
                link(v.tensor_scalar(den[:, :, 0], e[:, :, 0], 1.0, None, ALU.add))
                link(v.reciprocal(w[:, :, 0], den[:, :, 0]))
                link(v.tensor_tensor(w[:, :, 1], e[:, :, 0], w[:, :, 0], ALU.mult))
                return at + count[0]

            def x_of(b):
                return x_in[:, b & 1, :, :] if isinstance(b, int) else x_in[:, v.snap(b & 1), :, :]

            def stats_a(b):
                v.wait_ge(x_loaded, 16 * b + 16)
                stats(b, x_of(b), norm_a, norm_order_a, ve_a)

            def stats_b(b):
                v.wait_ge(x1_done, TT * b + TT)
                stats(b, x1, norm_b, norm_order_b, ve_b)

            def normalise_a(b):
                normalise(b, x_of(b), xna, norm_a, norm_order_a, sd_a, xn_a)

            def normalise_b(b):
                normalise(b, x1, xnb, norm_b, norm_order_b, sd_b, xn_b)

            def best_sets(b):
                v.wait_ge(sc_ready, b + 1)
                link, count = counter(order_a, ORDER_A * b)
                link(v.tensor_tensor(sc[:, :, :], p_sc[:, 0:TT * N].rearrange("p (i n) -> p i n", i=TT),
                                     penalty[:, :, :], ALU.add), carrier=2)
                two_best(b, sc, iota_set, N, best_a, bidx_a, order_a, ORDER_A, 1, gap_a,
                         oh[:, 0, :, :], oh[:, 1, :, :])

            def best_experts(b):
                v.wait_ge(lg_ready, b + 1)
                link, count = counter(order_b, ORDER_B * b)
                link(v.tensor_copy(lg[:, :, :], p_lg[:, 0:TT * E].rearrange("p (i n) -> p i n", i=TT)), carrier=3)
                two_best(b, lg, iota_exp, E, best_b, bidx_b, order_b, ORDER_B, 1, gap_b,
                         sel[:, :, 0:E], sel[:, :, E:2 * E])

            def mixture_weights(b):
                at = softmax_two(b, best_a, order_a, ORDER_A, 1 + 3, eg_a)
                link, count = counter(order_a, ORDER_A * b + at)
                for s in range(2):
                    ins = v.tensor_tensor(oh[:, s, :, :], oh[:, s, :, :],
                                          best_a[5][:, :, s:s + 1].to_broadcast([P, TT, N]), ALU.mult)
                link(ins)
                v.tensor_tensor(wd[:, :, 0:N], oh[:, 0, :, :], oh[:, 1, :, :], ALU.add).then_inc(wd_done, 1)
                assert at + 1 == ORDER_A

            def routing_table(b):
                at = softmax_two(b, best_b, order_b, ORDER_B, 1 + 3, eg_b)
                v.tensor_tensor(sel[:, :, 2 * E:3 * E], sel[:, :, E:2 * E], sel[:, :, 0:E], ALU.subtract)
                v.tensor_copy(sel[:, :, 3 * E:3 * E + 2], best_b[5][:, :, :]).then_inc(sel_done, 1)
                assert at == ORDER_B

            def residual(b):
                if not isinstance(b, int) or b:
                    v.wait_ge(x1_out, 16 * b)
                x = x_of(b)
                for i in range(TT):
                    v.wait_ge(mix_ready, TT * b + (i + 1))
                    v.tensor_tensor(x1[:, i, :], (p_mix, pt[4])[i % 2][:, :], x[:, i, :], ALU.add)\
                     .then_inc(x1_done, 1)

            stats_a(0)
            v.wait_ge(desc_ready, 1)
            v.tensor_copy(desc_t[:, :, :], pt[4][:, 0:KC * N].rearrange("p (k n) -> p k n", k=KC))
            v.tensor_copy(bq_col[:, :], pt[4][:, KC * N:KC * N + KC]).then_inc(desc_done, 1)
            normalise_a(0)
            allowed_sets()
            v.wait_ge(sw_ready, 1)
            v.tensor_copy(score_w[:, :, :], p_sc[:, 0:KC * N].rearrange("p (k n) -> p k n", k=KC))
            v.tensor_copy(score_b[:, :], p_sc[0:1, KC * N:KC * N + N]).then_inc(sw_done, 1)
            best_sets(0)
            mixture_weights(0)
            for bk in range(4):
                small_lo_part(bk)
            residual(0)
            for bk in range(4, 6):
                small_lo_part(bk)
            v.wait_ge(small_t, 7)
            v.tensor_copy(wg_t[:, :, :], pt[2][:, 0:KC * E].rearrange("p (k n) -> p k n", k=KC)).then_inc(small_lo, 1)
            stats_a(1)
            normalise_a(1)
            stats_b(0)
            normalise_b(0)

            def turn(b, last):
                best_sets(b)
                if not last:
                    stats_a(b + 1)
                mixture_weights(b)
                best_experts(b - 1)
                residual(b)
                if not last:
                    normalise_a(b + 1)
                stats_b(b)
                routing_table(b - 1)
                normalise_b(b)

            with v.Fori(1, B - 1) as b:
                turn(b, False)
            turn(B - 1, True)
            for k in range(KC):
                v.wait_ge(first_hi, k + 1)
                v.tensor_tensor(xt_lo[:, k, :], xt_raw[:, k, :], xt_hi[:, k, :].bitcast(f32), ALU.subtract)\
                 .then_inc(first_lo, 1)
            best_experts(B - 1)
            routing_table(B - 1)


def build_ffn(nc, out, scratch, keep):
    w_scr, x1_scr, xt_scr, sel_scr = scratch
    A13h, A13l, B2h, B2l, xt_raw, xt_hi, xt_lo = keep
    with ExitStack() as ctx:
        def sb(name, shape, dt=f32):
            return ctx.enter_context(nc.sbuf_tensor(name, shape, dt))

        def sem(name):
            return ctx.enter_context(nc.semaphore(name))

        def pair(name, shape, dt=f32):
            return [sb(f"{name}{j}", shape, dt) for j in range(2)]

        up_raw, dn_raw = pair("up_raw", [P, UPC]), pair("dn_raw", [P, DNC])
        up_hi, up_lo = pair("up_hi", [P, UPC], f32r), pair("up_lo", [P, UPC], f32r)
        dn_hi, dn_lo = pair("dn_hi", [P, DNC], f32r), pair("dn_lo", [P, DNC], f32r)
        am_hi = sb("am_hi", [P, 2, 2, AC, S], f32r)
        am_lo = sb("am_lo", [P, 2, 2, AC, S], f32r)
        mask_a = sb("mask_a", [P, 2, AC, S])
        mask_g = sb("mask_g", [P, 2, AC, S])
        rw = sb("rw", [P, 2, S])
        gate0, gate1 = pair("gate0_", [P, S]), pair("gate1_", [P, S])
        pq, sq = pair("pq", [P, S]), pair("sq", [P, S])
        p_hi, p_lo = pair("p_hi", [P, S], f32r), pair("p_lo", [P, S], f32r)
        s_hi, s_lo = pair("s_hi", [P, S], f32r), pair("s_lo", [P, S], f32r)
        g_hi, g_lo = p_hi, p_lo
        credit = sb("credit", [P, 16])
        acc = sb("acc", [P, TT, H])
        g_acc = sb("g_acc", [P, 2, AC, S])

        x1p = [ctx.enter_context(nc.psum_tensor(f"x1p{j}", [P, S], f32)) for j in range(2)]
        x3p = [ctx.enter_context(nc.psum_tensor(f"x3p{j}", [P, S], f32)) for j in range(2)]
        dp = [ctx.enter_context(nc.psum_tensor(f"dp{i}", [P, 512], f32)) for i in range(4)]

        up_in = [sem(f"up_in{j}") for j in range(2)]
        dn_in = [sem(f"dn_in{j}") for j in range(2)]
        up_hi_done = [sem(f"up_hi_done{j}") for j in range(2)]
        dn_hi_done = [sem(f"dn_hi_done{j}") for j in range(2)]
        up_ready = [sem(f"up_ready{j}") for j in range(2)]
        dn_ready = [sem(f"dn_ready{j}") for j in range(2)]
        xt_in, xt_hi_done, xt_ready = sem("xt_in"), sem("xt_hi_done"), sem("xt_ready")
        rw_in, mask_a_in, mask_g_in, acc_in = sem("rw_in"), sem("mask_a_in"), sem("mask_g_in"), sem("acc_in")
        dp_ready, dp_free = sem("dp_ready"), sem("dp_free")
        ah_done, al_done = sem("ah_done"), sem("al_done")
        am0, am1 = sem("am0"), sem("am1")
        x1a, x3a, x1b, x3b = sem("x1a"), sem("x3a"), sem("x1b"), sem("x3b")
        silu0, silu1 = sem("silu0"), sem("silu1")
        p_done, q_done, s_done = sem("p_done"), sem("q_done"), sem("s_done")
        ph, sh, sl = sem("ph"), sem("sh"), sem("sl")
        g_done, gh, gl = sem("g_done"), sem("gh"), sem("gl")
        g_zero, y_out = sem("g_zero"), sem("y_out")
        gate, g_prod = sem("gate"), sem("g_prod")

        block = ctx.enter_context(nc.Block())

        DPB = 8 * GROUPS + 4

        def dp_base(b, g, last=False):
            late = isinstance(g, int) and g == GROUPS - 1 and not last
            return b * DPB + g * 8 + (8 if late else 4)

        def blocks(eng, body):
            with eng.Fori(0, B - 1) as b:
                body(b, False)
            body(B - 1, True)

        def pairs_of_chunks(eng, group, b, last):
            group(b, 0, last)
            with eng.Fori(1, GROUPS - 1) as g:
                group(b, g, last)
            group(b, GROUPS - 1, last)

        @block.sync
        def _(sp):
            def val(x):
                return x if isinstance(x, int) else sp.snap(x)

            def load(sem_free, need, dst, src, sem_in):
                need = val(need)
                sp.wait_ge(sem_free, need)
                sp.dma_start(dst, src).then_inc(sem_in, 16)

            def load_masks(dst, which, b, sem_in):
                for s, m in enumerate(which):
                    for e in range(E):
                        a, r0 = e // (P // R), (e % (P // R)) * R
                        sp.dma_start(dst[r0:r0 + R, s, a, :], sel_scr[b, m * E + e, :].partition_broadcast(R))\
                          .then_inc(sem_in, 16)

            def load_rw(b):
                for s in range(2):
                    sp.dma_start(rw[:, s, :], sel_scr[b, 3 * E + s, :].partition_broadcast(P)).then_inc(rw_in, 16)

            def group(b, g):
                q1 = val(b * GROUPS + g + 1)
                load(up_ready[1], q1, up_raw[1][:, :], w_scr[val(2 * g + 1), :, 0:UPC], up_in[1])
                for j in range(2):
                    load(dn_ready[j], q1, dn_raw[j][:, :], w_scr[val(2 * g + j), :, UPC:WCOLS], dn_in[j])
                load(up_ready[0], q1, up_raw[0][:, :], w_scr[val(2 * g + 2), :, 0:UPC], up_in[0])

            def body(b, last):
                group(b, 0)
                need = val(AC * b + 1)
                sp.wait_ge(gl, need)
                load_masks(mask_g, (1, 2), b, mask_g_in)
                load(y_out, 16 * b + 16, acc[:, :, :], x1_scr[b, :, :, :], acc_in)
                if not last:
                    load(xt_ready, KC * b + (KC + 1), xt_raw[:, :, :], xt_scr[val(b + 1), :, :, :], xt_in)
                    need0, need1 = val(2 * AC * b + 2 * AC), val(2 * AC * b + (2 * AC + 1))
                    nxt = val(b + 1)
                    sp.wait_ge(am0, need0)
                    sp.wait_ge(am1, need1)
                    load_masks(mask_a, (0, 2), nxt, mask_a_in)
                with sp.Fori(1, GROUPS) as g:
                    group(b, g)
                if not last:
                    nxt = val(b + 1)
                    need = val(FC * b + (FC + 2))
                    sp.wait_ge(q_done, need)
                    load_rw(nxt)

            sp.dma_start(up_raw[0][:, :], w_scr[0, :, 0:UPC]).then_inc(up_in[0], 16)
            load_masks(mask_a, (0, 2), 0, mask_a_in)
            load_rw(0)
            blocks(sp, body)

        @block.gpsimd
        def _(pool):
            def up_split(j, n):
                pool.wait_ge(up_hi_done[j], n)
                pool.tensor_tensor(up_lo[j][:, :], up_raw[j][:, :], up_hi[j][:, :].bitcast(f32), ALU.subtract)\
                    .then_inc(up_ready[j], 1)

            def dn_split(j, n):
                pool.wait_ge(dn_hi_done[j], n)
                pool.tensor_tensor(dn_lo[j][:, :], dn_raw[j][:, :], dn_hi[j][:, :].bitcast(f32), ALU.subtract)\
                    .then_inc(dn_ready[j], 1)

            def masked(b):
                pool.wait_ge(mask_a_in, 32 * E * (b + 1))
                for t in range(2 * AC):
                    m, a = t // AC, t % AC
                    pool.wait_ge(al_done, b * 2 * AC + (t + 1))
                    for dst, src in ((am_hi, gate0), (am_lo, gate1)):
                        ins = pool.tensor_tensor(dst[:, m, 1, a, :], src[t % 2][:, :], mask_a[:, 1, a, :], ALU.mult)
                    ins.then_inc(am1, 1)

            def body(b, last):
                with pool.Fori(0, GROUPS) as g:
                    q = b * GROUPS + g
                    up_split(1, q + 1)
                    up_split(0, q + 2)
                    dn_split(0, q + 1)
                    dn_split(1, q + 1)
                if not last:
                    masked(b + 1)

            up_split(0, 1)
            masked(0)
            blocks(pool, body)

        @block.scalar
        def _(act):
            def up_split(j, n):
                act.wait_ge(up_in[j], 16 * n)
                act.activation(up_hi[j][:, :], up_raw[j][:, :], ACT.Copy).then_inc(up_hi_done[j], 1)

            def dn_split(j, n):
                act.wait_ge(dn_in[j], 16 * n)
                act.activation(dn_hi[j][:, :], dn_raw[j][:, :], ACT.Copy).then_inc(dn_hi_done[j], 1)

            def xt_split(b):
                act.wait_ge(xt_in, 16 * b)
                for k in range(KC):
                    act.activation(xt_hi[:, k, :], xt_raw[:, k, :], ACT.Copy).then_inc(xt_hi_done, 1)

            def a_split(b, at):
                for t in range(2 * AC):
                    act.wait_ge(dp_ready, at + (t + 1))
                    if t >= 2:
                        act.wait_ge(am0, b * 2 * AC + (t - 1))
                        act.wait_ge(am1, b * 2 * AC + t)
                    act.activation(gate0[t % 2][:, :].bitcast(f32r), dp[t][:, :], ACT.Copy).then_inc(ah_done, 1)

            def group(b, g, last):
                q = b * GROUPS + g
                n = q * 2
                final = isinstance(g, int) and g == GROUPS - 1
                for j in range(2):
                    act.wait_ge(x1a, n + (j + 1))
                    act.activation(gate0[j][:, :], x1p[j][:, :], ACT.Silu).then_inc(silu0, 1)
                    if j == 0:
                        up_split(1, q + 1)
                    elif final and not last:
                        act.wait_ge(x3a, n + 2)
                        xt_split(b + 1)
                    act.wait_ge(x1b, n + (j + 1))
                    act.activation(gate1[j][:, :], x1p[j][:, :], ACT.Silu).then_inc(silu1, 1)
                    if j == 0:
                        act.wait_ge(dp_ready, b * DPB + g * 8 + 4)
                    act.wait_ge(p_done, n + (j + 1))
                    act.activation(p_hi[j][:, :], pq[j][:, :], ACT.Copy).then_inc(ph, 1)
                    act.wait_ge(s_done, n + (j + 1))
                    act.activation(s_hi[j][:, :], sq[j][:, :], ACT.Copy).then_inc(sh, 1)
                    if j == 0:
                        up_split(0, q + 2)
                        dn_split(0, q + 1)
                        dn_split(1, q + 1)

            def body(b, last):
                act.wait_ge(am1, 2 * AC * b + (2 * AC + 1))
                pairs_of_chunks(act, group, b, last)
                if not last:
                    a_split(b + 1, b * DPB + (DPB - 8))
                for a in range(AC):
                    act.wait_ge(g_done, b * AC + (a + 1))
                    act.activation(g_hi[a][:, :], g_acc[:, 0, a, :], ACT.Copy).then_inc(gh, 1)
                act.wait_ge(dp_free, dp_base(b, GROUPS - 1, last) + 12)
                act.dma_start(out[b, :, :].rearrange("(i p) h -> p i h", p=P), acc[:, :, :]).then_inc(y_out, 16)

            up_split(0, 1)
            a_split(0, 0)
            blocks(act, body)
            act.wait_ge(y_out, 16 * B + 16)

        @block.vector
        def _(v):
            for x, (s, n) in enumerate(((dp_free, 4), (silu1, 2), (q_done, 2), (up_ready[1], 1), (dn_ready[0], 1),
                                        (dn_ready[1], 1), (gl, 1), (xt_ready, KC + 1), (am1, 1),
                                        (xt_hi_done, KC), (y_out, 16))):
                v.memset(credit[:, x:x + 1], 0.0).then_inc(s, n)

            def zero_g():
                v.memset(g_acc[:, :, :, :], 0.0).then_inc(g_zero, 1)

            def xt_split(b):
                for k in range(KC):
                    v.wait_ge(xt_hi_done, b * KC + (k + 1))
                    v.tensor_tensor(xt_lo[:, k, :], xt_raw[:, k, :], xt_hi[:, k, :].bitcast(f32), ALU.subtract)\
                     .then_inc(xt_ready, 1)

            def masked(b):
                v.wait_ge(mask_a_in, 32 * E * (b + 1))
                for t in range(2 * AC):
                    m, a = t // AC, t % AC
                    v.wait_ge(ah_done, b * 2 * AC + (t + 1))
                    v.tensor_tensor(gate1[t % 2][:, :].bitcast(f32r), dp[t][:, :], gate0[t % 2][:, :], ALU.subtract)\
                     .then_inc(dp_free, 1)
                    v.tensor_tensor(am_hi[:, m, 0, a, :], gate0[t % 2][:, :], mask_a[:, 0, a, :], ALU.mult)\
                     .then_inc(al_done, 1)
                    v.wait_ge(al_done, b * 2 * AC + (t + 1))
                    v.tensor_tensor(am_lo[:, m, 0, a, :], gate1[t % 2][:, :], mask_a[:, 0, a, :], ALU.mult)\
                     .then_inc(am0, 1)

            def g_adds(at):
                for t in range(2 * AC):
                    v.wait_ge(dp_ready, at + (t + 1))
                    to = g_acc[:, t // AC, t % AC, :]
                    v.tensor_tensor(to, dp[t][:, :], to, ALU.add).then_inc(dp_free, 1)

            def out_adds(at):
                for i in range(TT):
                    v.wait_ge(dp_ready, at + (2 * AC + i + 1))
                    v.tensor_tensor(acc[:, i, :], dp[i][:, :], acc[:, i, :], ALU.add).then_inc(dp_free, 1)

            def group(b, g, last):
                n = b * FC + g * 2
                final = isinstance(g, int) and g == GROUPS - 1
                for j in range(2):
                    v.wait_ge(silu0, n + (j + 1))
                    v.tensor_tensor(gate0[j][:, :], gate0[j][:, :], rw[:, 0, :], ALU.mult).then_inc(gate, 1)
                    v.wait_ge(gate, n * 2 + (2 * j + 1))
                    v.wait_ge(x3a, n + (j + 1))
                    v.tensor_tensor(pq[j][:, :], x3p[j][:, :], gate0[j][:, :], ALU.mult).then_inc(p_done, 1)
                    if j == 0 and not (isinstance(g, int) and g == 0):
                        v.wait_ge(g_zero, b + 1)
                        v.wait_ge(acc_in, 16 * (b + 1))
                        g_adds(b * DPB + g * 8 - 4)
                        out_adds(b * DPB + g * 8 - 4)
                    if j == 1 and final and not last:
                        xt_split(b + 1)
                    v.wait_ge(silu1, n + (j + 3))
                    v.tensor_tensor(gate1[j][:, :], gate1[j][:, :], rw[:, 1, :], ALU.mult).then_inc(gate, 1)
                    v.wait_ge(gate, n * 2 + (2 * j + 2))
                    v.wait_ge(x3b, n + (j + 1))
                    v.tensor_tensor(sq[j][:, :], x3p[j][:, :], gate1[j][:, :], ALU.mult).then_inc(q_done, 1)
                    v.wait_ge(q_done, n + (j + 3))
                    v.tensor_tensor(sq[j][:, :], sq[j][:, :], pq[j][:, :], ALU.add).then_inc(s_done, 1)
                    v.wait_ge(ph, n + (j + 1))
                    v.tensor_tensor(p_lo[j][:, :], pq[j][:, :], p_hi[j][:, :].bitcast(f32), ALU.subtract)
                    v.wait_ge(sh, n + (j + 1))
                    v.tensor_tensor(s_lo[j][:, :], sq[j][:, :], s_hi[j][:, :].bitcast(f32), ALU.subtract)\
                     .then_inc(sl, 1)

            def body(b, last):
                v.wait_ge(rw_in, 32 * (b + 1))
                pairs_of_chunks(v, group, b, last)
                if not last:
                    masked(b + 1)
                at = dp_base(b, GROUPS - 1, last)
                g_adds(at)
                v.wait_ge(mask_g_in, 32 * E * (b + 1))
                v.wait_ge(dp_free, at + 8)
                for a in range(AC):
                    v.tensor_tensor(g_acc[:, 0, a, :], g_acc[:, 0, a, :], mask_g[:, 0, a, :], ALU.mult)
                    v.tensor_tensor(g_acc[:, 1, a, :], g_acc[:, 1, a, :], mask_g[:, 1, a, :], ALU.mult)\
                     .then_inc(g_prod, 1)
                for a in range(AC):
                    v.wait_ge(g_prod, b * AC + (a + 1))
                    v.tensor_tensor(g_acc[:, 0, a, :], g_acc[:, 0, a, :], g_acc[:, 1, a, :], ALU.subtract)\
                     .then_inc(g_done, 1)
                for a in range(AC):
                    v.wait_ge(gh, b * AC + (a + 1))
                    v.tensor_tensor(g_lo[a][:, :], g_acc[:, 0, a, :], g_hi[a][:, :].bitcast(f32), ALU.subtract)\
                     .then_inc(gl, 1)
                out_adds(at)
                if not last:
                    v.wait_ge(gl, AC * b + (AC + 1))
                    zero_g()

            zero_g()
            masked(0)
            blocks(v, body)

        @block.tensor
        def _(pe):
            def product(dst, operands, start, stop):
                for x, (lh, ll, rh, rl) in enumerate(operands):
                    for y, (lhs, rhs) in enumerate(((lh, rh), (lh, rl), (ll, rh))):
                        mm = pe.matmul(dst, lhs, rhs, start=start and x == 0 and y == 0,
                                       stop=stop and x == len(operands) - 1 and y == 2, skip_group_check=True)
                return mm

            def base(j, m):
                at = m * KC * P
                return [(up_hi[j][:, at + k * P:at + (k + 1) * P], up_lo[j][:, at + k * P:at + (k + 1) * P],
                         xt_hi[:, k, :], xt_lo[:, k, :]) for k in range(KC)]

            def lora(j, m, s):
                at = LORA + m * AC * P
                return [(up_hi[j][:, at + a * P:at + (a + 1) * P], up_lo[j][:, at + a * P:at + (a + 1) * P],
                         am_hi[:, m, s, a, :], am_lo[:, m, s, a, :]) for a in range(AC)]

            def a_tiles(b, at):
                for t in range(2 * AC):
                    m, a = t // AC, t % AC
                    pe.wait_ge(dp_free, at + (t + 1))
                    c = slice(a * P, (a + 1) * P)
                    for k in range(KC):
                        if t == 0:
                            pe.wait_ge(xt_ready, b * KC + (k + 2))
                        mm = product(dp[t][:, :], [(A13h[:, m, k, c], A13l[:, m, k, c], xt_hi[:, k, :],
                                                    xt_lo[:, k, :])], k == 0, k == KC - 1)
                    mm.then_inc(dp_ready, 1)

            def down(b, g, at, finish=False):
                q = b * GROUPS + g
                for j in range(2):
                    pe.wait_ge(dn_ready[j], q + 2)
                pe.wait_ge(sl, q * 2 + 2)
                for t in range(2 * AC):
                    pe.wait_ge(dp_free, at + (t + 1))
                    c = slice(H + (t % AC) * P, H + (t % AC + 1) * P)
                    hi, lo = (s_hi, s_lo) if t < AC else (p_hi, p_lo)
                    product(dp[t][:, :], [(dn_hi[j][:, c], dn_lo[j][:, c], hi[j][:, :], lo[j][:, :])
                                          for j in range(2)], True, True).then_inc(dp_ready, 1)
                for i in range(TT):
                    pe.wait_ge(dp_free, at + (2 * AC + i + 1))
                    c = slice(i * P, (i + 1) * P)
                    mm = product(dp[i][:, :], [(s_hi[j][:, c], s_lo[j][:, c], dn_hi[j][:, 0:H], dn_lo[j][:, 0:H])
                                               for j in range(2)], True, not finish)
                    if not finish:
                        mm.then_inc(dp_ready, 1)
                if finish:
                    pe.wait_ge(gl, AC * b + (AC + 1))
                    for i in range(TT):
                        c = slice(i * P, (i + 1) * P)
                        product(dp[i][:, :], [(g_hi[a][:, c], g_lo[a][:, c], B2h[:, a, :], B2l[:, a, :])
                                              for a in range(AC)], False, True).then_inc(dp_ready, 1)

            def group(b, g, last):
                q = b * GROUPS + g
                n = q * 2
                opening = isinstance(g, int) and g == 0
                for j in range(2):
                    pe.wait_ge(up_ready[j], q + (1 + j))
                    pe.wait_ge(silu1, n + (j + 1))
                    product(x1p[j][:, :], base(j, 0), True, False)
                    if opening and j == 0:
                        pe.wait_ge(am0, b * 2 * AC + 2 * AC)
                    product(x1p[j][:, :], lora(j, 0, 0), False, True).then_inc(x1a, 1)
                    pe.wait_ge(q_done, n + (j + 1))
                    product(x3p[j][:, :], base(j, 1) + lora(j, 1, 0), True, True).then_inc(x3a, 1)
                    if j == 0 and not opening:
                        down(b, g - 1, b * DPB + g * 8 - 4)
                    pe.wait_ge(silu0, n + (j + 1))
                    if opening and j == 0:
                        pe.wait_ge(am1, b * 2 * AC + (2 * AC + 1))
                    product(x1p[j][:, :], lora(j, 0, 1), False, True).then_inc(x1b, 1)
                    pe.wait_ge(p_done, n + (j + 1))
                    product(x3p[j][:, :], lora(j, 1, 1), False, True).then_inc(x3b, 1)

            def body(b, last):
                pairs_of_chunks(pe, group, b, last)
                if not last:
                    a_tiles(b + 1, b * DPB + (DPB - 8))
                down(b, GROUPS - 1, dp_base(b, GROUPS - 1, last), finish=True)

            a_tiles(0, 0)
            blocks(pe, body)


def build(nc, io, out):
    def dram(name, shape):
        return nc.dram_tensor(name, shape, f32, kind="Internal").ap()

    scratch = (dram("w_scr", (FC + 1, P, WCOLS)), dram("x1_scr", (B, P, TT, H)),
               dram("xt_scr", (B, P, KC, S)), dram("sel_scr", (B, SELR, S)))
    with (nc.sbuf_tensor("A13h", [P, 2, KC, ER], f32r) as A13h, nc.sbuf_tensor("A13l", [P, 2, KC, ER], f32r) as A13l,
          nc.sbuf_tensor("B2h", [P, AC, H], f32r) as B2h, nc.sbuf_tensor("B2l", [P, AC, H], f32r) as B2l,
          nc.sbuf_tensor("xt_raw", [P, KC, S], f32) as xt_raw, nc.sbuf_tensor("xt_hi", [P, KC, S], f32r) as xt_hi,
          nc.sbuf_tensor("xt_lo", [P, KC, S], f32r) as xt_lo):
        keep = (A13h, A13l, B2h, B2l, xt_raw, xt_hi, xt_lo)
        build_front(nc, io, scratch, keep)
        build_ffn(nc, out, scratch, keep)


_INS = {"x": "x", "ctx_2048": "ctx", "itok_Sx4_0_63": "tok", "L0_xattn_desc_router": "desc", "L0_xattn_W_q": "W_q",
        "L0_xattn_b_q": "b_q", "L0_ffn_Wg": "Wg", "L0_ffn_W1": "W1", "L0_ffn_W2": "W2", "L0_ffn_W3": "W3",
        "L0_ffn_A1": "A1", "L0_ffn_B1": "B1", "L0_ffn_A2": "A2", "L0_ffn_B2": "B2", "L0_ffn_A3": "A3",
        "L0_ffn_B3": "B3"}


def kernel(**inputs):
    import numpy as _np
    import concourse.bacc as _bacc
    from concourse import mybir as _mybir
    from concourse.bass_utils import run_bass_kernel_spmd as _run

    nc = _bacc.Bacc("TRN2", target_bir_lowering=False, num_devices=1)
    arrays, io = {}, {}
    for name, short in _INS.items():
        a = _np.ascontiguousarray(inputs[name])
        arrays[f"in_{name}"] = a
        io[short] = nc.dram_tensor(f"in_{name}", a.shape, _mybir.dt.from_np(a.dtype), kind="ExternalInput").ap()
    out = nc.dram_tensor("out_0", (B, S, H), _mybir.dt.float32, kind="ExternalOutput").ap()
    build(nc, io, out)
    r = _run(nc, [arrays], core_ids=[0])
    return r.results[0]["out_0"]
```
